# Optimizing a Trainium2 kernel written in Bass

```python
import numpy as np
import jax
import jax.numpy as jnp

def _softmax(x, axis=-1):
    return jax.nn.softmax(x, axis=axis)

def _gelu(x):
    return jax.nn.gelu(x, approximate=True)

def _silu(x):
    return jax.nn.silu(x)

def _sigmoid(x):
    return jax.nn.sigmoid(x)

def _layernorm(x, axis=-1, eps=1e-05):
    m = jnp.mean(x, axis=axis, keepdims=True)
    v = jnp.var(x, axis=axis, keepdims=True)
    return (x - m) / jnp.sqrt(v + eps)

def _scatter_add(tgt, idx, src, axis=0):
    return tgt.at[idx].add(src)

def _segment_sum(src, seg, n):
    return jax.ops.segment_sum(src, seg, n)
kernel_name = 'mk_macaron_d1_jaxref_r8_06feff'

def setup_inputs(seed: int=0):
    np.random.seed(seed)
    _w = jnp.asarray

    def _L0_attn_setup():
        import jax, jax.numpy as jnp
        import numpy as np
        B, S, D = (4, 256, 128)
        key = jax.random.key(seed)
        k1, k2, k3, k4 = jax.random.split(key, 4)
        x = jax.random.normal(k1, (B, S, D), dtype=jnp.float32)
        Qw = jax.random.normal(k2, (D, D), dtype=jnp.float32) / 40
        Kw = jax.random.normal(k3, (D, D), dtype=jnp.float32) / 40
        Vw = jax.random.normal(k4, (D, D), dtype=jnp.float32) / 40
        return {'x': x, 'Qw': Qw, 'Kw': Kw, 'Vw': Vw}
    _L0_attn_in = _L0_attn_setup()

    def _L0_ffn_setup():
        import jax, jax.numpy as jnp
        import numpy as np
        H = 128
        I = 64
        IS = 128
        E = 16
        G = 4
        TOPK_G = 2
        TOPK = 4
        SCALE = 2.5
        B, S = (2, 128)

        def _relu2(x):
            r = jax.nn.relu(x)
            return r * r

        def _route(scores, bias_corr):
            T = scores.shape[0]
            s_choice = scores + bias_corr
            gs = s_choice.reshape(T, G, E // G)
            group_scores = jnp.sum(jax.lax.top_k(gs, 2)[0], axis=-1)
            gidx = jax.lax.top_k(group_scores, TOPK_G)[1]
            gmask = jnp.sum(jax.nn.one_hot(gidx, G, dtype=scores.dtype), axis=1)
            smask = jnp.repeat(gmask, E // G, axis=1)
            masked = jnp.where(smask > 0, s_choice, 0.0)
            topk_idx = jax.lax.top_k(masked, TOPK)[1]
            topk_w = jnp.take_along_axis(scores, topk_idx, axis=1)
            topk_w = topk_w / (jnp.sum(topk_w, axis=-1, keepdims=True) + 1e-20)
            topk_w = topk_w * SCALE
            return (topk_idx, topk_w)
        key = jax.random.key(seed)
        ks = jax.random.split(key, 8)
        sd = 0.02
        return {'hidden_states': jax.random.normal(ks[0], (B, S, H), jnp.float32), 'Wg': jax.random.normal(ks[1], (E, H), jnp.float32) * sd, 'bias_corr': jax.random.normal(ks[2], (E,), jnp.float32) * 0.01, 'W1': jax.random.normal(ks[3], (E, I, H), jnp.float32) * sd, 'W2': jax.random.normal(ks[4], (E, H, I), jnp.float32) * sd, 'Ws1': jax.random.normal(ks[5], (IS, H), jnp.float32) * sd, 'Ws2': jax.random.normal(ks[6], (H, IS), jnp.float32) * sd}
    _L0_ffn_in = _L0_ffn_setup()
    _d = {'L0_attn_x': _L0_attn_in['x'], 'L0_attn_Qw': _L0_attn_in['Qw'], 'L0_attn_Kw': _L0_attn_in['Kw'], 'L0_attn_Vw': _L0_attn_in['Vw'], 'L0_ffn_Wg': _L0_ffn_in['Wg'], 'L0_ffn_bias_corr': _L0_ffn_in['bias_corr'], 'L0_ffn_W1': _L0_ffn_in['W1'], 'L0_ffn_W2': _L0_ffn_in['W2'], 'L0_ffn_Ws1': _L0_ffn_in['Ws1'], 'L0_ffn_Ws2': _L0_ffn_in['Ws2']}
    _x0 = _d['L0_attn_x']
    _d['L0_attn_x'] = jax.random.normal(jax.random.fold_in(jax.random.key(seed), 1), (8, 1024, 128), dtype=_x0.dtype)
    del _x0
    return _d

def reference(L0_attn_x, L0_attn_Qw, L0_attn_Kw, L0_attn_Vw, L0_ffn_Wg, L0_ffn_bias_corr, L0_ffn_W1, L0_ffn_W2, L0_ffn_Ws1, L0_ffn_Ws2):

    def _L0_attn_ref(x, Qw, Kw, Vw):
        import jax, jax.numpy as jnp
        import numpy as np
        B, S, D = (4, 256, 128)
        Q = x @ Qw
        K = x @ Kw
        V = x @ Vw
        d = x.shape[-1]
        S_len = x.shape[-2]
        mask = jnp.where(jnp.tril(jnp.ones((S_len, S_len), dtype=x.dtype)) == 0, -jnp.inf, 0.0).astype(x.dtype)
        scores = jnp.einsum('bqd,bkd->bqk', Q, K) / jnp.sqrt(jnp.asarray(d, x.dtype))
        scores = scores + mask
        attn = jax.nn.softmax(scores, axis=-1)
        return jnp.einsum('bqk,bkd->bqd', attn, V)

    def _L0_ffn_ref(hidden_states, Wg, bias_corr, W1, W2, Ws1, Ws2):
        import jax, jax.numpy as jnp
        import numpy as np
        H = 128
        I = 64
        IS = 128
        E = 16
        G = 4
        TOPK_G = 2
        TOPK = 4
        SCALE = 2.5
        B, S = (2, 128)

        def _relu2(x):
            r = jax.nn.relu(x)
            return r * r

        def _route(scores, bias_corr):
            T = scores.shape[0]
            s_choice = scores + bias_corr
            gs = s_choice.reshape(T, G, E // G)
            group_scores = jnp.sum(jax.lax.top_k(gs, 2)[0], axis=-1)
            gidx = jax.lax.top_k(group_scores, TOPK_G)[1]
            gmask = jnp.sum(jax.nn.one_hot(gidx, G, dtype=scores.dtype), axis=1)
            smask = jnp.repeat(gmask, E // G, axis=1)
            masked = jnp.where(smask > 0, s_choice, 0.0)
            topk_idx = jax.lax.top_k(masked, TOPK)[1]
            topk_w = jnp.take_along_axis(scores, topk_idx, axis=1)
            topk_w = topk_w / (jnp.sum(topk_w, axis=-1, keepdims=True) + 1e-20)
            topk_w = topk_w * SCALE
            return (topk_idx, topk_w)
        b, s, h = hidden_states.shape
        flat = hidden_states.reshape(-1, h)
        T = flat.shape[0]
        logits = flat.astype(jnp.float32) @ Wg.T
        scores = jax.nn.sigmoid(logits)
        topk_idx, topk_w = _route(scores, bias_corr)
        topk_w = topk_w.astype(hidden_states.dtype)
        cw = jnp.zeros((T, E), flat.dtype)
        cw = cw.at[jnp.arange(T)[:, None], topk_idx].add(topk_w)
        hid = _relu2(jnp.einsum('th,eih->eti', flat, W1))
        y = jnp.einsum('eti,ehi->eth', hid, W2)
        out = jnp.einsum('eth,te->th', y, cw)
        shared = _relu2(flat @ Ws1.T) @ Ws2.T
        return (out + shared).reshape(b, s, h)
    x = L0_attn_x
    x = x + 0.5 * _L0_ffn_ref(_layernorm(x, axis=-1), L0_ffn_Wg, L0_ffn_bias_corr, L0_ffn_W1, L0_ffn_W2, L0_ffn_Ws1, L0_ffn_Ws2)
    x = x + _L0_attn_ref(_layernorm(x, axis=-1), L0_attn_Qw, L0_attn_Kw, L0_attn_Vw)
    x = x + 0.5 * _L0_ffn_ref(_layernorm(x, axis=-1), L0_ffn_Wg, L0_ffn_bias_corr, L0_ffn_W1, L0_ffn_W2, L0_ffn_Ws1, L0_ffn_Ws2)
    return x

_drawn_inputs = setup_inputs


def setup_inputs(seed=0):
    import zlib

    import numpy as np

    out = dict(_drawn_inputs(seed))
    spreads = {}
    factors = {'L0_attn_Qw': 8.0,
     'L0_attn_Kw': 8.0,
     'L0_ffn_Wg': 5.266,
     'L0_ffn_bias_corr': 8.0,
     'L0_ffn_W1': 4.971,
     'L0_ffn_W2': 4.53,
     'L0_ffn_Ws1': 4.378,
     'L0_ffn_Ws2': 3.979}
    for name, (base, spread) in spreads.items():
        noise = np.random.default_rng([zlib.crc32(name.encode()), seed]).standard_normal(out[name].shape)
        drawn = base * np.exp(spread * noise) if base else spread * noise
        out[name] = jnp.asarray(drawn.astype(out[name].dtype))
    for name, factor in factors.items():
        out[name] = (out[name] * factor).astype(out[name].dtype)
    return out
```

```python
from contextlib import ExitStack

import concourse.bass as bass
from concourse import mybir

F32 = mybir.dt.float32
F32R = mybir.dt.float32r
BF16 = mybir.dt.bfloat16
ALU = mybir.AluOpType
ACT = mybir.ActivationFunctionType
AX = mybir.AxisListType

P = 128
LN_EPS = 1e-5
TOPK_G = 2
TOPK = 4
N_GRP = 4
ROUTE_SCALE = 2.5
ROUTE_EPS = 1e-20
ABSENT = -3.0e38
PICKED = 3.0e38
MASKED = -1.0e30


class FfnSems:
    def __init__(self, sem, tag):
        self.stat = sem(tag + "stat")
        self.var_done = sem(tag + "var_done")
        self.rstd_done = sem(tag + "rstd_done")
        self.xn_done = sem(tag + "xn_done")
        self.xnT_done = sem(tag + "xnT_done")
        self.xhi_done = sem(tag + "xhi_done")
        self.xlo_done = sem(tag + "xlo_done")
        self.lg_done = sem(tag + "lg_done")
        self.sig_done = sem(tag + "sig_done")
        self.route = sem(tag + "route")
        self.cw_done = sem(tag + "cw_done")
        self.cwT_done = sem(tag + "cwT_done")
        self.cwT_copied = sem(tag + "cwT_copied")
        self.up_done = sem(tag + "up_done")
        self.cb_done = sem(tag + "cb_done")
        self.relu_done = sem(tag + "relu_done")
        self.sq_done = sem(tag + "sq_done")
        self.gate_done = sem(tag + "gate_done")
        self.down_done = sem(tag + "down_done")
        self.oT_copied = sem(tag + "oT_copied")
        self.oTr_done = sem(tag + "oTr_done")
        self.res_done = sem(tag + "res_done")


class AttentionSems:
    def __init__(self, sem):
        self.stat = sem("a_stat")
        self.var_done = sem("a_var_done")
        self.rstd_done = sem("a_rstd_done")
        self.zn_done = sem("a_zn_done")
        self.t_done = sem("a_t_done")
        self.zhi_done = sem("a_zhi_done")
        self.zlo_done = sem("a_zlo_done")
        self.q_done = sem("a_q_done")
        self.qhi_done = sem("a_qhi_done")
        self.qlo_done = sem("a_qlo_done")
        self.sc_done = sem("a_sc_done")
        self.max_done = sem("a_max_done")
        self.exp_done = sem("a_exp_done")
        self.tp_done = sem("a_tp_done")
        self.pT_done = sem("a_pT_done")
        self.u_done = sem("a_u_done")
        self.uT_done = sem("a_uT_done")
        self.out_done = sem("a_out_done")
        self.rinv_done = sem("a_rinv_done")
        self.fin_done = sem("a_fin_done")


def macaron_kernel(nc, x, Qw, Kw, Vw, Wg, bias_corr, W1, W2, Ws1, Ws2, out):
    B, S, D = x.shape
    E, I, _ = W1.shape
    NT = B * S // P
    TG = 4
    GT = TG * P
    NG = NT // TG
    NC = E * I // P
    NCH = NC + 1
    QT = S // P
    EG = E // N_GRP
    UN = 2
    LAG = 3
    RING = 3
    PR = 4
    PADT = QT
    assert D == P and Ws1.shape[0] == P and (NCH * UN) % RING == 0 and E * 2 <= P

    x_v = x.rearrange("b (t p) d -> p (b t) d", p=P)
    out_v = out.rearrange("b (t p) d -> p (b t) d", p=P)

    with ExitStack() as ctx:
        def sb(name, shape, dt=F32):
            return ctx.enter_context(nc.sbuf_tensor(name, shape, dt))

        def sem(name):
            return ctx.enter_context(nc.semaphore(name))

        x_sb = sb("x_sb", [P, NT + PADT, D])
        w1_raw = sb("w1_raw", [P, NCH, D])
        w2_raw = sb("w2_raw", [P, NCH, P])
        qk_raw = sb("qk_raw", [P, 2, D])
        wg_raw = sb("wg_raw", [E, D])
        w1_hi = sb("w1_hi", [P, NCH, P], F32R)
        w1_lo = sb("w1_lo", [P, NCH, P], F32R)
        w2T = sb("w2T", [P, NCH, D])
        wg_hi = sb("wg_hi", [P, E], F32R)
        wg_lo = sb("wg_lo", [P, E], F32R)
        qkT = sb("qkT", [P, 2, P])
        m_hi = sb("m_hi", [P, P], F32R)
        m_f = sb("m_f", [P, P])
        m_lo = sb("m_lo", [P, P], F32R)
        vw = sb("vw", [P, D])
        bias_bc = sb("bias_bc", [P, E])
        ident = sb("ident", [P, P])
        identb = sb("identb", [P, P], BF16)
        maskb = sb("maskb", [P, P], BF16)
        sel_f = sb("sel_f", [P, NC, P])
        sel = sb("sel", [P, NC, P], F32R)
        earlier = sb("earlier", [P, TG, N_GRP, N_GRP])
        tick = sb("tick", [P, 1])
        neg_half = sb("neg_half", [P, QT])
        bn = sb("bn", [P, QT, 6])
        mv = sb("mv", [P, QT, 2])
        rstd = sb("rstd", [P, QT])
        xn = sb("xn", [P, UN, TG, D])
        x_hi = sb("x_hi", [P, UN, GT], F32R)
        x_lo = sb("x_lo", [P, UN, GT], F32R)
        scores = sb("scores", [P, TG, E])
        choice = sb("choice", [P, TG, E])
        pair_hi = sb("pair_hi", [P, TG * N_GRP, 2])
        pair_lo = sb("pair_lo", [P, TG * N_GRP, 2])
        top1 = sb("top1", [P, TG * N_GRP])
        top2a = sb("top2a", [P, TG * N_GRP])
        top2b = sb("top2b", [P, TG * N_GRP])
        gscore = sb("gscore", [P, TG, N_GRP])
        beats = sb("beats", [P, TG, N_GRP, N_GRP])
        beats_eq = sb("beats_eq", [P, TG, N_GRP, N_GRP])
        grank = sb("grank", [P, TG, N_GRP])
        gmask = sb("gmask", [P, TG, N_GRP])
        masked = sb("masked", [P, TG, E])
        cand = sb("cand", [P, TG, E + 4])
        top8 = sb("top8", [P, TG, 8])
        wanted = sb("wanted", [P, TG, 8])
        marked = sb("marked", [P, TG, E + 4])
        chosen = sb("chosen", [P, TG, E])
        wsum = sb("wsum", [P, TG])
        wrec = sb("wrec", [P, TG])
        cw = sb("cw", [P, TG, E])
        cw_pad = sb("cw_pad", [P, TG, P])
        cwT = sb("cwT", [P, UN, GT], F32R)
        act = sb("act", [P, RING, GT])
        act2 = sb("act2", [P, RING, GT])
        gated = sb("gated", [P, RING, GT])
        oT = sb("oT", [P, GT])
        zn = sb("zn", [P, UN, QT, D])
        z_hi = sb("z_hi", [P, UN, S], F32R)
        z_lo = sb("z_lo", [P, UN, S], F32R)
        q_hi = sb("q_hi", [P, UN, S], F32R)
        q_lo = sb("q_lo", [P, UN, S], F32R)
        nmax = sb("nmax", [P, UN, QT])
        rsum = sb("rsum", [P, UN, QT])
        rinv = sb("rinv", [P, 2, QT // 2])
        prob = sb("prob", [P, PR, S])
        HQ = QT // 2
        pT = [sb("pT_a", [P, HQ, HQ * P]), sb("pT_b", [P, QT, HQ * P])]
        uT = sb("uT", [P, 2, HQ * P])

        psum = ctx.enter_context(nc.psum_tensor("psum", [P, 8, 512], F32))
        up_ps = [psum[:, 0, :], psum[:, 1, :]]
        cb_ps = [psum[:, 2, :], psum[:, 3, :]]
        o_ps = [psum[:, 4, :], psum[:, 5, :]]
        tr_ps = psum[:, 6, :]
        lg_ps = psum[:, 7, :]
        sc_ps = [psum[:, 0:2, :].rearrange("p a n -> p (a n)"), psum[:, 2:4, :].rearrange("p a n -> p (a n)")]
        tp_ps = psum[:, 4:6, :].rearrange("p a n -> p (a n)")
        misc_ps = psum[:, 6, :]
        u_ps = psum[:, 7, :]

        x_in = [sem(f"x_in{g}") for g in range(4)]
        x_rest = sem("x_rest")
        w1_in, w2_in, small_in = sem("w1_in"), sem("w2_in"), sem("small_in")
        const_done, self_done = sem("const_done"), sem("const_self")
        sel_done = sem("sel_done")
        wt_done, wt_hi, wt_free = sem("wt_done"), sem("wt_hi"), sem("wt_free")
        m_done, m_copied, m_hi_done, m_ready = sem("m_done"), sem("m_copied"), sem("m_hi_done"), sem("m_ready")
        stored = sem("stored")

        FF = [FfnSems(sem, "f0_"), FfnSems(sem, "f1_")]
        AT = AttentionSems(sem)

        def wait(eng, s, value):
            if not (isinstance(value, int) and value <= 0):
                eng.wait_ge(s, value)

        block = ctx.enter_context(nc.Block())

        @block.sync
        def _(sp):
            for g in range(2):
                sp.dma_start(x_sb[:, TG * g:TG * (g + 1), :], x_v[:, TG * g:TG * (g + 1), :]).then_inc(x_in[g], 16)
            w1_rows = W1.rearrange("e i h -> (e i) h").rearrange("(c p) h -> p c h", p=P)
            sp.dma_start(w1_raw[:, 0:NC, :], w1_rows).then_inc(w1_in, 16)
            sp.dma_start(w1_raw[:, NC, :], Ws1).then_inc(w1_in, 16)
            for g in range(2, 4):
                sp.dma_start(x_sb[:, TG * g:TG * (g + 1), :], x_v[:, TG * g:TG * (g + 1), :]).then_inc(x_in[g], 16)
            sp.dma_start(x_sb[:, 4 * TG:NT, :], x_v[:, 4 * TG:NT, :]).then_inc(x_rest, 16)

            def store(g):
                sp.wait_ge(FF[1].res_done, g + 1)
                sp.dma_start(out_v[:, bass.ds(g * TG, TG), :], x_sb[:, bass.ds(g * TG, TG), :]).then_inc(stored, 16)

            with sp.Fori(0, NG) as g:
                store(g)
            sp.wait_ge(stored, 16 * NG)

        @block.gpsimd
        def _(pool):
            nc.gpsimd.memset(ident[:], 0.0).then_inc(self_done, 1)
            nc.gpsimd.memset(sel_f[:], 0.0).then_inc(self_done, 1)
            nc.gpsimd.memset(maskb[:], 0.0).then_inc(self_done, 1)
            nc.gpsimd.memset(earlier[:], 1.0).then_inc(self_done, 1)
            nc.gpsimd.memset(neg_half[:], -0.5).then_inc(const_done, 1)
            pool.wait_ge(self_done, 4)
            nc.gpsimd.affine_select(out=ident[:], in_=ident[:], compare_op=ALU.not_equal, fill=1.0, base=0,
                                    pattern=[[-1, P]], channel_multiplier=1).then_inc(const_done, 1)
            nc.gpsimd.affine_select(out=maskb[:], in_=maskb[:], compare_op=ALU.is_ge, fill=MASKED, base=0,
                                    pattern=[[-1, P]], channel_multiplier=1).then_inc(const_done, 1)
            sel_view = sel_f[:].rearrange("p c (j i) -> p c j i", j=P // I)
            pattern = [[-(P // I), NC], [-1, P // I], [0, I]]
            nc.gpsimd.affine_select(out=sel_view, in_=sel_view, compare_op=ALU.not_equal, fill=1.0, base=0,
                                    pattern=pattern, channel_multiplier=1).then_inc(self_done, 1)
            pool.wait_ge(self_done, 5)
            nc.gpsimd.affine_select(out=sel_view, in_=sel_view, compare_op=ALU.not_equal, fill=1.0, base=-E,
                                    pattern=pattern, channel_multiplier=1).then_inc(sel_done, 1)
            nc.gpsimd.affine_select(out=earlier[:], in_=earlier[:], compare_op=ALU.is_gt, fill=0.0, base=0,
                                    pattern=[[0, TG], [1, N_GRP], [-1, N_GRP]], channel_multiplier=0).then_inc(const_done, 1)
            nc.gpsimd.memset(x_sb[:, NT:NT + PADT, :], 0.0).then_inc(const_done, 1)

            def inv_std(S_, n, tiles):
                pool.wait_ge(S_.var_done, n + 1)
                nc.gpsimd.tensor_tensor(rstd[:, 0:tiles], mv[:, 0:tiles, 1], neg_half[:, 0:tiles],
                                        ALU.pow).then_inc(S_.rstd_done, 1)

            for phase in range(3):
                if phase == 1:
                    with pool.Fori(0, B + 1) as n:
                        inv_std(AT, n, QT)
                else:
                    with pool.Fori(0, NG + 2) as n:
                        inv_std(FF[phase // 2], n, TG)

        @block.scalar
        def _(sc):
            copy = lambda o, i, scale=1.0: nc.scalar.activation(o, i, ACT.Copy, scale=scale)

            sc.dma_start(w2_raw[:, 0:NC, :].rearrange("h c (j i) -> h (c j) i", i=I),
                         W2.rearrange("e h i -> h e i")).then_inc(w2_in, 16)
            sc.dma_start(w2_raw[:, NC, :], Ws2).then_inc(w2_in, 16)
            sc.dma_start(wg_raw[:], Wg).then_inc(small_in, 16)
            sc.dma_start(bias_bc[:], bias_corr.rearrange("(a e) -> a e", a=1).broadcast_to([P, E])).then_inc(small_in, 16)
            sc.dma_start(qk_raw[:, 0, :], Qw).then_inc(small_in, 16)
            sc.dma_start(qk_raw[:, 1, :], Kw).then_inc(small_in, 16)
            sc.dma_start(vw[:], Vw).then_inc(small_in, 16)

            sc.wait_ge(const_done, 5)
            copy(identb[:], ident[:]).then_inc(m_copied, 1)
            for w in range(5):
                sc.wait_ge(wt_done, w + 1)
                src = up_ps[w % 2]
                if w < 2:
                    copy(w1_hi[:, 4 * w:4 * w + 4, :].rearrange("p c n -> p (c n)"), src).then_inc(wt_hi, 1)
                elif w < 4:
                    copy(w2T[:, 4 * (w - 2):4 * (w - 2) + 4, :].rearrange("p c n -> p (c n)"), src).then_inc(wt_hi, 1)
                else:
                    copy(w1_hi[:, NC, :], src[:, 0:P])
                    copy(w2T[:, NC, :], src[:, P:2 * P])
                    copy(qkT[:].rearrange("p c n -> p (c n)"), src[:, 2 * P:4 * P]).then_inc(wt_hi, 1)
            sc.wait_ge(wt_done, 6)
            copy(wg_hi[:], up_ps[1][:, 0:E]).then_inc(wt_hi, 1)
            sc.wait_ge(m_done, 1)
            copy(m_f[:], cb_ps[0][:, 0:P], scale=float(D) ** -0.5).then_inc(m_copied, 1)
            sc.wait_ge(m_copied, 2)
            copy(m_hi[:], m_f[:]).then_inc(m_hi_done, 1)

            def ffn(F):
                def x_hi_copy(g, u):
                    sc.wait_ge(F.xnT_done, g + 1)
                    copy(x_hi[:, u, :], tr_ps).then_inc(F.xhi_done, 1)

                def sigmoid(g):
                    sc.wait_ge(F.lg_done, g + 1)
                    wait(sc, F.cw_done, g)
                    nc.scalar.activation(scores[:].rearrange("p t e -> p (t e)"), lg_ps[:, 0:TG * E],
                                         ACT.Sigmoid).then_inc(F.sig_done, 1)

                def cwT_copy(g, u):
                    sc.wait_ge(F.cwT_done, g + 1)
                    copy(cwT[:, u, :], lg_ps).then_inc(F.cwT_copied, 1)

                def oT_copy(g, u):
                    sc.wait_ge(F.down_done, NCH * (g + 1))
                    wait(sc, F.oTr_done, g)
                    copy(oT[:], o_ps[u]).then_inc(F.oT_copied, 1)

                def square(g, k, n, j):
                    sc.wait_ge(F.relu_done, n + 1)
                    if k < NC:
                        wait(sc, F.gate_done, NC * g + k + 1 - RING if k >= RING else NC * (g - 1) + NC - (RING - 1 - k))
                        nc.scalar.activation(act2[:, j % RING, :], act[:, j % RING, :], ACT.Square).then_inc(F.sq_done, 1)
                    else:
                        wait(sc, F.down_done, n + 1 - RING)
                        nc.scalar.activation(gated[:, j % RING, :], act[:, j % RING, :], ACT.Square).then_inc(F.sq_done, 1)

                def body(i, first):
                    for u in range(UN):
                        g = i * UN + u
                        for k in range(NCH):
                            j = u * NCH + k
                            n = i * (UN * NCH) + j
                            sc.wait_ge(F.up_done, n + 1)
                            wait(sc, F.sq_done, n + 1 - RING)
                            nc.scalar.activation(act[:, j % RING, :], up_ps[j % 2], ACT.Relu).then_inc(F.relu_done, 1)
                            if k > 0:
                                square(g, k - 1, n - 1, j - 1)
                            elif not (first and u == 0):
                                square(g - 1, NC, n - 1, (j - 1) % (UN * NCH))
                            if k == 0 and not (first and u == 0):
                                cwT_copy(g, u)
                            if k == 1:
                                x_hi_copy(g + 1, 1 - u)
                            if k == 3 and not (first and u == 0):
                                oT_copy(g - 1, 1 - u)
                            if k == 5:
                                sigmoid(g + 1)

                x_hi_copy(0, 0)
                sigmoid(0)
                cwT_copy(0, 0)
                body(0, True)
                with sc.Fori(1, NG // UN) as i:
                    body(i, False)
                square(NG - 1, NC, NCH * NG - 1, UN * NCH - 1)
                oT_copy(NG - 1, (NG - 1) % UN)

            def attention():
                A = AT

                def z_hi_copy(b, u, half):
                    sc.wait_ge(A.t_done, 2 * b + half + 1)
                    copy(z_hi[:, u, half * 512:half * 512 + 512], misc_ps).then_inc(A.zhi_done, 1)

                def q_hi_copy(b, u, half):
                    sc.wait_ge(A.q_done, 2 * b + half + 1)
                    copy(q_hi[:, u, half * 512:half * 512 + 512], misc_ps).then_inc(A.qhi_done, 1)

                def uT_copy(b, half):
                    sc.wait_ge(A.u_done, 2 * b + half + 1)
                    wait(sc, A.out_done, 2 * (b - 1) + half + 1)
                    copy(uT[:, half, :], u_ps).then_inc(A.uT_done, 1)

                def exp(b, t, u):
                    m = QT * b + t
                    sc.wait_ge(A.max_done, m + 1)
                    wait(sc, A.tp_done, m + 1 - PR)
                    w = (t + 1) * P
                    nc.scalar.activation(prob[:, t % PR, 0:w], sc_ps[t % 2][:, 0:w], ACT.Exp, bias=nmax[:, u, t:t + 1],
                                         accum_out=rsum[:, u, t:t + 1]).then_inc(A.exp_done, 1)

                def pT_copy(b, t):
                    m = QT * b + t
                    half, q0 = t // HQ, (t % HQ) * P
                    sc.wait_ge(A.tp_done, m + 1)
                    if t % HQ == 0:
                        wait(sc, A.u_done, 2 * (b - 1) + half + 1)
                    copy(pT[half][:, 0:t + 1, q0:q0 + P],
                         tp_ps[:, 0:(t + 1) * P].rearrange("p (k q) -> p k q", q=P)).then_inc(A.pT_done, 1)

                def body(i, first):
                    for u in range(UN):
                        b = i * UN + u
                        old = not (first and u == 0)
                        for t in range(QT):
                            exp(b, t, u)
                            if t >= 2:
                                pT_copy(b, t - 2)
                            elif old:
                                pT_copy(b - 1, QT + t - 2)
                            if t == 0:
                                if old:
                                    uT_copy(b - 1, 0)
                                q_hi_copy(b, u, 1)
                            if t == 3 and old:
                                uT_copy(b - 1, 1)
                            if t == 5:
                                z_hi_copy(b + 1, 1 - u, 0)
                            if t == 6:
                                z_hi_copy(b + 1, 1 - u, 1)
                            if t == 7:
                                q_hi_copy(b + 1, 1 - u, 0)

                z_hi_copy(0, 0, 0)
                z_hi_copy(0, 0, 1)
                q_hi_copy(0, 0, 0)
                body(0, True)
                with sc.Fori(1, B // UN) as i:
                    body(i, False)
                pT_copy(B - 1, QT - 2)
                uT_copy(B - 1, 0)
                pT_copy(B - 1, QT - 1)
                uT_copy(B - 1, 1)

            ffn(FF[0])
            attention()
            ffn(FF[1])

        @block.vector
        def _(v):
            tt = nc.vector.tensor_tensor
            f32 = lambda ap: ap.bitcast(F32)

            v.wait_ge(const_done, 5)
            nc.vector.memset(cand[:, :, E:E + 4], ABSENT).then_inc(FF[0].stat, 1)
            nc.vector.memset(wanted[:, :, 4:8], ABSENT).then_inc(FF[0].stat, 1)
            nc.vector.memset(cw_pad[:], 0.0).then_inc(FF[0].stat, 1)
            n_const = 3
            v.wait_ge(FF[0].stat, n_const)

            def lo_parts(w):
                v.wait_ge(wt_hi, w + 1)
                src = up_ps[w % 2]
                if w < 2:
                    cs = slice(4 * w, 4 * w + 4)
                    flat = lambda a: a[:, cs, :].rearrange("p c n -> p (c n)")
                    tt(flat(w1_lo), src, f32(flat(w1_hi)), ALU.subtract).then_inc(wt_free, 1)
                elif w == 4:
                    tt(w1_lo[:, NC, :], src[:, 0:P], f32(w1_hi[:, NC, :]), ALU.subtract).then_inc(wt_free, 1)
                elif w == 5:
                    tt(wg_lo[:], src[:, 0:E], f32(wg_hi[:]), ALU.subtract).then_inc(wt_free, 1)

            def carry():
                nc.vector.memset(tick[:], 0.0)

            def norm_stats(S_, n, tile0, tiles, base):
                wait(v, S_.zn_done if S_ is AT else S_.xn_done, n)
                for t in range(tiles):
                    nc.vector.bn_stats(bn[:, t, :], x_sb[:, bass.ds(tile0 + t, 1), :].rearrange("p t d -> p (t d)")).then_inc(S_.stat, 1)
                v.wait_ge(S_.stat, base + n * (2 * tiles) + tiles)
                carry()
                for t in range(tiles):
                    nc.vector.bn_aggr(mv[:, t, :], bn[:, t, :]).then_inc(S_.stat, 1)
                v.wait_ge(S_.stat, base + (n + 1) * (2 * tiles))
                nc.vector.tensor_scalar(mv[:, 0:tiles, 1], mv[:, 0:tiles, 1], LN_EPS, None, ALU.add).then_inc(S_.var_done, 1)

            def norm_apply(S_, n, tile0, tiles, dst, done):
                v.wait_ge(S_.rstd_done, n + 1)
                for t in range(tiles):
                    ins = nc.vector.tensor_scalar(dst[:, t, :], x_sb[:, bass.ds(tile0 + t, 1), :].rearrange("p t d -> p (t d)"),
                                                  mv[:, t, 0:1], rstd[:, t:t + 1], ALU.subtract, ALU.mult)
                ins.then_inc(done, 1)

            F0 = FF[0]

            def ffn(F, phase):
                base = n_const if phase == 0 else 0
                N_ROUTE = 32

                def norm(g, u):
                    norm_stats(F, g, g * TG, TG, base)
                    norm_apply(F, g, g * TG, TG, xn[:, u], F.xn_done)

                def x_lo_part(g, u):
                    v.wait_ge(F.xhi_done, g + 1)
                    tt(x_lo[:, u, :], tr_ps, f32(x_hi[:, u, :]), ALU.subtract).then_inc(F.xlo_done, 1)

                def route(g, part):
                    step0 = g * N_ROUTE
                    at = [{0: 0, 1: 13, 2: 22}[part]]

                    def do(ins):
                        ins.then_inc(F.route, 1)
                        at[0] += 1

                    def settled():
                        v.wait_ge(F.route, step0 + at[0])

                    if part == 0:
                        v.wait_ge(F.sig_done, g + 1)
                        do(tt(choice[:], scores[:], bias_bc[:].unsqueeze(1).to_broadcast([P, TG, E]), ALU.add))
                        settled()
                        ch = choice[:].rearrange("p t (g e) -> p (t g) e", e=EG)
                        do(tt(pair_hi[:], ch[:, :, 0:2], ch[:, :, 2:4], ALU.max))
                        do(tt(pair_lo[:], ch[:, :, 0:2], ch[:, :, 2:4], ALU.min))
                        settled()
                        do(tt(top1[:], pair_hi[:, :, 0], pair_hi[:, :, 1], ALU.max))
                        do(tt(top2a[:], pair_hi[:, :, 0], pair_hi[:, :, 1], ALU.min))
                        do(tt(top2b[:], pair_lo[:, :, 0], pair_lo[:, :, 1], ALU.max))
                        settled()
                        do(tt(top2a[:], top2a[:], top2b[:], ALU.max))
                        settled()
                        do(tt(gscore[:].rearrange("p t g -> p (t g)"), top1[:], top2a[:], ALU.add))
                        settled()
                        gj = gscore[:].unsqueeze(2).to_broadcast([P, TG, N_GRP, N_GRP])
                        gg = gscore[:].unsqueeze(3).to_broadcast([P, TG, N_GRP, N_GRP])
                        do(tt(beats[:], gj, gg, ALU.is_gt))
                        do(tt(beats_eq[:], gj, gg, ALU.is_equal))
                        settled()
                        do(tt(beats_eq[:], beats_eq[:], earlier[:], ALU.mult))
                        settled()
                        do(tt(beats[:], beats[:], beats_eq[:], ALU.add))
                        settled()
                        do(nc.vector.tensor_reduce(grank[:].rearrange("p t g -> p (t g)"),
                                                   beats[:].rearrange("p t g j -> p (t g) j"), AX.X, ALU.add))
                    if part == 1:
                        settled()
                        do(nc.vector.tensor_scalar(gmask[:], grank[:], TOPK_G - 0.5, None, ALU.is_lt))
                        settled()
                        do(tt(masked[:].rearrange("p t (g e) -> p (t g) e", e=EG), choice[:].rearrange("p t (g e) -> p (t g) e", e=EG),
                              gmask[:].rearrange("p t g -> p (t g)").unsqueeze(2).to_broadcast([P, TG * N_GRP, EG]), ALU.mult))
                        settled()
                        do(nc.vector.tensor_scalar(cand[:, :, 0:E], masked[:], 0.0, None, ALU.add))
                        settled()
                        carry()
                        for t in range(TG):
                            do(nc.vector.max(top8[:, t, :], cand[:, t, 0:E]))
                        settled()
                        do(nc.vector.tensor_copy(wanted[:, :, 0:TOPK], top8[:, :, 0:TOPK]))
                        settled()
                        carry()
                        do(nc.vector.match_replace(marked[:, 0, :], wanted[:, 0, :], cand[:, 0, :], PICKED))
                    if part == 2:
                        for t in range(1, TG):
                            do(nc.vector.match_replace(marked[:, t, :], wanted[:, t, :], cand[:, t, :], PICKED))
                        settled()
                        do(tt(chosen[:], marked[:, :, 0:E], cand[:, :, 0:E], ALU.not_equal))
                        settled()
                        do(tt(chosen[:], chosen[:], scores[:], ALU.mult))
                        settled()
                        do(nc.vector.tensor_reduce(wsum[:], chosen[:], AX.X, ALU.add))
                        settled()
                        do(nc.vector.tensor_scalar(wsum[:], wsum[:], ROUTE_EPS, None, ALU.add))
                        settled()
                        do(nc.vector.reciprocal(wrec[:], wsum[:]))
                        settled()
                        do(nc.vector.scalar_tensor_tensor(cw[:], chosen[:], ROUTE_SCALE,
                                                          wrec[:].unsqueeze(2).to_broadcast([P, TG, E]), ALU.mult, ALU.mult))
                        settled()
                        wait(v, F.cwT_done, g)
                        do(nc.vector.tensor_copy(cw_pad[:, :, 0:E].bitcast(F32R), cw[:]))
                        settled()
                        last = tt(cw_pad[:, :, E:2 * E], cw[:], cw_pad[:, :, 0:E], ALU.subtract)
                        last.then_inc(F.cw_done, 1)
                        assert at[0] == N_ROUTE

                def gate(g, k, n, j, par):
                    v.wait_ge(F.sq_done, n + 1)
                    v.wait_ge(F.cb_done, NC * g + k + 1)
                    wait(v, F.down_done, n + 1 - RING)
                    tt(gated[:, j % RING, :], cb_ps[par], act2[:, j % RING, :], ALU.mult).then_inc(F.gate_done, 1)

                def residual(g):
                    v.wait_ge(F.oTr_done, g + 1)
                    xs = x_sb[:, bass.ds(g * TG, TG), :].rearrange("p t d -> p (t d)")
                    nc.vector.scalar_tensor_tensor(xs, tr_ps, 0.5, xs, ALU.mult, ALU.add).then_inc(F.res_done, 1)

                def body(i, first):
                    for u in range(UN):
                        g = i * UN + u
                        for k in range(NCH):
                            j = u * NCH + k
                            n = i * (UN * NCH) + j
                            if k < NC:
                                gate(g, k, n, j, (u * NC + k) % 2)
                            if k == 1:
                                x_lo_part(g + 1, 1 - u)
                            if k in (4, 5, 6):
                                route(g + 1, k - 4)
                            if k == 6 and not (first and u == 0):
                                residual(g - 1)
                            if k == 7:
                                if phase == 0 and first:
                                    v.wait_ge(x_in[2 + u], 16)
                                norm_stats(F, g + 2, (g + 2) * TG, TG, base)
                            if k == 8:
                                norm_apply(F, g + 2, (g + 2) * TG, TG, xn[:, u], F.xn_done)

                if phase == 0:
                    v.wait_ge(x_in[0], 16)
                else:
                    v.wait_ge(AT.fin_done, 2 * B)
                norm(0, 0)
                if phase == 0:
                    for w in range(6):
                        lo_parts(w)
                    v.wait_ge(sel_done, 1)
                    nc.vector.tensor_copy(sel[:], sel_f[:]).then_inc(wt_free, 1)
                    v.wait_ge(small_in, 16 * 5)
                x_lo_part(0, 0)
                for part in range(3):
                    route(0, part)
                if phase == 0:
                    v.wait_ge(x_in[1], 16)
                norm(1, 1)
                if phase == 0:
                    v.wait_ge(m_hi_done, 1)
                    tt(m_lo[:], m_f[:], f32(m_hi[:]), ALU.subtract).then_inc(m_ready, 1)
                body(0, True)
                if phase == 0:
                    v.wait_ge(x_rest, 16)
                with v.Fori(1, NG // UN) as i:
                    body(i, False)
                residual(NG - 1)

            def attention():
                A = AT

                def z_lo_part(b, u, half):
                    v.wait_ge(A.zhi_done, 2 * b + half + 1)
                    cs = slice(half * 512, half * 512 + 512)
                    tt(z_lo[:, u, cs], misc_ps, f32(z_hi[:, u, cs]), ALU.subtract).then_inc(A.zlo_done, 1)

                def q_lo_part(b, u, half):
                    v.wait_ge(A.qhi_done, 2 * b + half + 1)
                    cs = slice(half * 512, half * 512 + 512)
                    tt(q_lo[:, u, cs], misc_ps, f32(q_hi[:, u, cs]), ALU.subtract).then_inc(A.qlo_done, 1)

                def row_max(b, t, u):
                    v.wait_ge(A.sc_done, QT * b + t + 1)
                    nc.vector.tensor_reduce(nmax[:, u, t:t + 1], sc_ps[t % 2][:, 0:(t + 1) * P], AX.X, ALU.max,
                                            negate=True).then_inc(A.max_done, 1)

                def norm(b, u):
                    wait(v, A.u_done, 2 * (b - 1))
                    norm_stats(A, b, b * QT, QT, 0)
                    norm_apply(A, b, b * QT, QT, zn[:, u], A.zn_done)

                def finish(b, u, half):
                    v.wait_ge(A.exp_done, QT * b + HQ * (half + 1))
                    nc.vector.reciprocal(rinv[:, half, :], rsum[:, u, half * HQ:(half + 1) * HQ]).then_inc(A.rinv_done, 1)
                    v.wait_ge(A.rinv_done, 2 * b + half + 1)
                    v.wait_ge(A.out_done, 2 * b + half + 1)
                    for t in range(HQ):
                        xs = x_sb[:, bass.ds(b * QT + half * HQ + t, 1), :].rearrange("p t d -> p (t d)")
                        ins = nc.vector.scalar_tensor_tensor(xs, misc_ps[:, t * P:(t + 1) * P], rinv[:, half, t:t + 1], xs,
                                                             ALU.mult, ALU.add)
                    ins.then_inc(A.fin_done, 1)

                def body(i, first):
                    for u in range(UN):
                        b = i * UN + u
                        old = not (first and u == 0)
                        for t in range(QT):
                            row_max(b, t, u)
                            if t == 0:
                                q_lo_part(b, u, 1)
                            if t == 2 and old:
                                finish(b - 1, 1 - u, 0)
                            if t == 3:
                                norm(b + 1, 1 - u)
                            if t == 4 and old:
                                finish(b - 1, 1 - u, 1)
                            if t == 5:
                                z_lo_part(b + 1, 1 - u, 0)
                            if t == 6:
                                z_lo_part(b + 1, 1 - u, 1)
                            if t == 7:
                                q_lo_part(b + 1, 1 - u, 0)

                v.wait_ge(FF[0].res_done, NG)
                norm(0, 0)
                z_lo_part(0, 0, 0)
                z_lo_part(0, 0, 1)
                q_lo_part(0, 0, 0)
                body(0, True)
                with v.Fori(1, B // UN) as i:
                    body(i, False)
                finish(B - 1, (B - 1) % UN, 0)
                finish(B - 1, (B - 1) % UN, 1)

            ffn(FF[0], 0)
            attention()
            ffn(FF[1], 1)

        @block.tensor
        def _(pe):
            mm = nc.tensor.matmul

            def split3(out_, l_hi, l_lo, r_hi, r_lo, start=True, stop=True):
                mm(out_, l_hi, r_hi, start=start, stop=False)
                mm(out_, l_hi, r_lo, start=False, stop=False)
                return mm(out_, l_lo, r_hi, start=False, stop=stop)

            pe.wait_ge(const_done, 5)
            pe.wait_ge(w1_in, 32)
            for w in range(6):
                dst = up_ps[w % 2]
                if w == 2:
                    pe.wait_ge(w2_in, 32)
                if w == 4:
                    pe.wait_ge(small_in, 16 * 5)
                if w >= 2:
                    pe.wait_ge(wt_hi, w - 1)
                    wait(pe, wt_free, {2: 1, 3: 2}.get(w, 0))
                if w < 2:
                    srcs = [w1_raw[:, 4 * w + c, :] for c in range(4)]
                elif w < 4:
                    srcs = [w2_raw[:, 4 * (w - 2) + c, :] for c in range(4)]
                elif w == 4:
                    srcs = [w1_raw[:, NC, :], w2_raw[:, NC, :], qk_raw[:, 0, :], qk_raw[:, 1, :]]
                else:
                    srcs = []
                    nc.tensor.transpose(dst[:, 0:E], wg_raw[:], ident[0:E, 0:E]).then_inc(wt_done, 1)
                for c, src in enumerate(srcs):
                    ins = nc.tensor.transpose(dst[:, c * P:(c + 1) * P], src, ident[:])
                if srcs:
                    ins.then_inc(wt_done, 1)
            pe.wait_ge(wt_hi, 5)
            mm(cb_ps[0][:, 0:P], qkT[:, 0, :], qkT[:, 1, :], start=True, stop=True).then_inc(m_done, 1)
            pe.wait_ge(wt_hi, 6)
            pe.wait_ge(wt_free, 5)
            pe.wait_ge(m_copied, 2)

            def ffn(F):
                def xn_transpose(g, u):
                    pe.wait_ge(F.xn_done, g + 1)
                    wait(pe, F.res_done, g - 2)
                    for t in range(TG):
                        ins = nc.tensor.transpose(tr_ps[:, t * P:(t + 1) * P], xn[:, u, t, :], ident[:])
                    ins.then_inc(F.xnT_done, 1)

                def logits(g, u):
                    pe.wait_ge(F.xlo_done, g + 1)
                    wait(pe, F.cwT_copied, g)
                    for t in range(TG):
                        ts = slice(t * P, (t + 1) * P)
                        ins = split3(lg_ps[:, t * E:(t + 1) * E], x_hi[:, u, ts], x_lo[:, u, ts], wg_hi[:], wg_lo[:])
                    ins.then_inc(F.lg_done, 1)

                def cw_transpose(g):
                    pe.wait_ge(F.cw_done, g + 1)
                    pe.wait_ge(F.sig_done, g + 1)
                    for t in range(TG):
                        ins = nc.tensor.transpose(lg_ps[:, t * P:(t + 1) * P], cw_pad[:, t, :], ident[:])
                    ins.then_inc(F.cwT_done, 1)

                def up(g, k, n, j, u):
                    if k == 0:
                        pe.wait_ge(F.xlo_done, g + 1)
                    wait(pe, F.relu_done, n - 1)
                    split3(up_ps[j % 2], w1_hi[:, k, :], w1_lo[:, k, :], x_hi[:, u, :], x_lo[:, u, :]).then_inc(F.up_done, 1)

                def spread(g, k, u):
                    if k == 0:
                        pe.wait_ge(F.cwT_copied, g + 1)
                    wait(pe, F.gate_done, NC * g + k - 1)
                    mm(cb_ps[(u * NC + k) % 2], sel[:, k, :], cwT[:, u, :], start=True, stop=True).then_inc(F.cb_done, 1)

                def down(g, k, n, j, u):
                    if k < NC:
                        pe.wait_ge(F.gate_done, NC * g + k + 1)
                    else:
                        pe.wait_ge(F.sq_done, n + 1)
                    if k == 0:
                        wait(pe, F.oT_copied, g - 1)
                    mm(o_ps[u], w2T[:, k, :], gated[:, j % RING, :], start=(k == 0), stop=(k == NCH - 1)).then_inc(F.down_done, 1)

                def o_transpose(g):
                    pe.wait_ge(F.oT_copied, g + 1)
                    wait(pe, F.xlo_done, g + 3 if not (isinstance(g, int) and g == NG - 1) else NG + 1)
                    for t in range(TG):
                        ins = nc.tensor.transpose(tr_ps[:, t * P:(t + 1) * P], oT[:, t * P:(t + 1) * P], ident[:])
                    ins.then_inc(F.oTr_done, 1)

                def body(i, first):
                    for u in range(UN):
                        g = i * UN + u
                        for k in range(NCH):
                            j = u * NCH + k
                            n = i * (UN * NCH) + j
                            up(g, k, n, j, u)
                            if k >= 1:
                                spread(g, k - 1, u)
                            if k == 0:
                                xn_transpose(g + 1, 1 - u)
                            if k == 3:
                                logits(g + 1, 1 - u)
                            if k == 6 and not (first and u == 0):
                                o_transpose(g - 1)
                            if k == 8:
                                cw_transpose(g + 1)
                            if k >= LAG:
                                down(g, k - LAG, n - LAG, j - LAG, u)
                            elif not (first and u == 0):
                                down(g - 1, NCH + k - LAG, n - LAG, (j - LAG) % (UN * NCH), 1 - u)

                xn_transpose(0, 0)
                logits(0, 0)
                cw_transpose(0)
                body(0, True)
                with pe.Fori(1, NG // UN) as i:
                    body(i, False)
                for k in range(NCH - LAG, NCH):
                    down(NG - 1, k, NCH * (NG - 1) + k, (UN - 1) * NCH + k, (NG - 1) % UN)
                o_transpose(NG - 1)

            def attention():
                A = AT

                def z_transpose(b, u, half):
                    if half == 0:
                        pe.wait_ge(A.zn_done, b + 1)
                        wait(pe, A.fin_done, 2 * (b - 1))
                        wait(pe, A.qlo_done, 2 * b)
                    else:
                        pe.wait_ge(A.zlo_done, 2 * b + 1)
                    for t in range(HQ):
                        ins = nc.tensor.transpose(misc_ps[:, t * P:(t + 1) * P], zn[:, u, half * HQ + t, :], ident[:])
                    ins.then_inc(A.t_done, 1)

                def q_product(b, u, half):
                    if half == 0:
                        pe.wait_ge(A.zlo_done, 2 * b + 2)
                    else:
                        pe.wait_ge(A.qlo_done, 2 * b + 1)
                    cs = slice(half * 512, half * 512 + 512)
                    split3(misc_ps, m_hi[:], m_lo[:], z_hi[:, u, cs], z_lo[:, u, cs]).then_inc(A.q_done, 1)

                def score(b, t, u):
                    if t % HQ == 0:
                        pe.wait_ge(A.qlo_done, 2 * b + t // HQ + 1)
                    wait(pe, A.exp_done, QT * b + t - 1)
                    dst = sc_ps[t % 2]
                    w = (t + 1) * P
                    qs = slice(t * P, (t + 1) * P)
                    for c0 in range(0, w, 512):
                        c1 = min(c0 + 512, w)
                        ins = split3(dst[:, c0:c1], q_hi[:, u, qs], q_lo[:, u, qs], z_hi[:, u, c0:c1], z_lo[:, u, c0:c1],
                                     stop=(c1 < w))
                    mm(dst[:, t * P:w], identb[:], maskb[:], start=False, stop=True).then_inc(A.sc_done, 1)

                def prob_transpose(b, t):
                    m = QT * b + t
                    pe.wait_ge(A.exp_done, m + 1)
                    wait(pe, A.pT_done, m)
                    for k in range(t + 1):
                        ins = nc.tensor.transpose(tp_ps[:, k * P:(k + 1) * P], prob[:, t % PR, k * P:(k + 1) * P], ident[:])
                    ins.then_inc(A.tp_done, 1)

                def mix(b, u, half, k0, k1):
                    last = (half + 1) * HQ
                    if k0 == 0:
                        pe.wait_ge(A.pT_done, QT * b + last)
                        wait(pe, A.uT_done, 2 * b + half)
                    for k in range(k0, k1):
                        q0 = max(0, k - half * HQ) * P
                        ins = mm(u_ps[:, q0:], zn[:, u, k, :], pT[half][:, k, q0:], start=(k == 0), stop=(k == last - 1))
                    if k1 == last:
                        ins.then_inc(A.u_done, 1)

                def values(b, half):
                    pe.wait_ge(A.uT_done, 2 * b + half + 1)
                    if half == 0:
                        wait(pe, A.qlo_done, min(2 * b + 4, 2 * B + 1) if isinstance(b, int) else 2 * b + 4)
                    else:
                        pe.wait_ge(A.fin_done, 2 * b + 1)
                    for t in range(HQ):
                        ins = mm(misc_ps[:, t * P:(t + 1) * P], uT[:, half, t * P:(t + 1) * P], vw[:], start=True, stop=True)
                    ins.then_inc(A.out_done, 1)

                def body(i, first):
                    for u in range(UN):
                        b = i * UN + u
                        old = not (first and u == 0)
                        for t in range(QT):
                            score(b, t, u)
                            if t >= 2:
                                prob_transpose(b, t - 2)
                            elif old:
                                prob_transpose(b - 1, QT + t - 2)
                            if t == 0:
                                q_product(b, u, 1)
                            if t == 1 and old:
                                values(b - 1, 0)
                            if t == 2 and old:
                                mix(b - 1, 1 - u, 1, 0, 3)
                            if t == 3 and old:
                                mix(b - 1, 1 - u, 1, 3, QT)
                            if t == 4 and old:
                                values(b - 1, 1)
                            if t == 5:
                                z_transpose(b + 1, 1 - u, 0)
                            if t == 6:
                                z_transpose(b + 1, 1 - u, 1)
                            if t == 7:
                                q_product(b + 1, 1 - u, 0)
                                mix(b, u, 0, 0, HQ)

                pe.wait_ge(m_ready, 1)
                pe.wait_ge(FF[0].res_done, NG)
                z_transpose(0, 0, 0)
                z_transpose(0, 0, 1)
                q_product(0, 0, 0)
                body(0, True)
                with pe.Fori(1, B // UN) as i:
                    body(i, False)
                b, u = B - 1, (B - 1) % UN
                prob_transpose(b, QT - 2)
                values(b, 0)
                prob_transpose(b, QT - 1)
                mix(b, u, 1, 0, QT)
                values(b, 1)

            ffn(FF[0])
            attention()
            pe.wait_ge(AT.fin_done, 2 * B)
            ffn(FF[1])


_INS = ["L0_attn_x", "L0_attn_Qw", "L0_attn_Kw", "L0_attn_Vw", "L0_ffn_Wg", "L0_ffn_bias_corr", "L0_ffn_W1", "L0_ffn_W2",
        "L0_ffn_Ws1", "L0_ffn_Ws2"]


def kernel(**inputs):
    import numpy as _np
    import concourse.bacc as _bacc
    from concourse import mybir as _mybir
    from concourse.bass_utils import run_bass_kernel_spmd as _run

    nc = _bacc.Bacc("TRN2", target_bir_lowering=False, num_devices=1)
    arrays, args = {}, []
    for name in _INS:
        a = _np.ascontiguousarray(inputs[name])
        arrays[f"in_{name}"] = a
        args.append(nc.dram_tensor(f"in_{name}", a.shape, _mybir.dt.from_np(a.dtype), kind="ExternalInput").ap())
    shape = inputs["L0_attn_x"].shape
    args.append(nc.dram_tensor("out", shape, _mybir.dt.float32, kind="ExternalOutput").ap())
    macaron_kernel(nc, *args)
    r = _run(nc, [arrays], core_ids=[0])
    return r.results[0]["out"]
```

```python
from contextlib import ExitStack

import concourse.bass as bass
from concourse import mybir

F32 = mybir.dt.float32
F32R = mybir.dt.float32r
BF16 = mybir.dt.bfloat16
I32 = mybir.dt.int32
ALU = mybir.AluOpType
ACT = mybir.ActivationFunctionType
AX = mybir.AxisListType

P = 128
LN_EPS = 1e-5
TOPK_G = 2
TOPK = 4
N_GRP = 4
ROUTE_SCALE = 2.5
ROUTE_EPS = 1e-20
ABSENT = -3.0e38
PICKED = 3.4028234663852886e38
RSQRT_GUESS = 0x5f3759df
MASKED = -1.0e30


class FfnSems:
    def __init__(self, sem, tag):
        self.stat = sem(tag + "stat")
        self.var_done = sem(tag + "var_done")
        self.rstd_done = sem(tag + "rstd_done")
        self.shift_done = sem(tag + "shift_done")
        self.xn_done = sem(tag + "xn_done")
        self.xn2_done = sem(tag + "xn2_done")
        self.xnT_done = sem(tag + "xnT_done")
        self.xf_done = sem(tag + "xf_done")
        self.xhi_done = sem(tag + "xhi_done")
        self.xlo_done = sem(tag + "xlo_done")
        self.lg_done = sem(tag + "lg_done")
        self.sig_done = sem(tag + "sig_done")
        self.route = sem(tag + "route")
        self.wsum_done = sem(tag + "wsum_done")
        self.norm_done = sem(tag + "norm_done")
        self.scw_done = sem(tag + "scw_done")
        self.scwT_done = sem(tag + "scwT_done")
        self.wT_done = sem(tag + "wT_done")
        self.w_stored = sem(tag + "w_stored")
        self.w_loaded = sem(tag + "w_loaded")
        self.up_done = sem(tag + "up_done")
        self.s_done = sem(tag + "s_done")
        self.sq_done = sem(tag + "sq_done")
        self.glo_done = sem(tag + "glo_done")
        self.down_done = sem(tag + "down_done")
        self.oT_copied = sem(tag + "oT_copied")
        self.oTr_done = sem(tag + "oTr_done")
        self.res_done = sem(tag + "res_done")


class AttentionSems:
    def __init__(self, sem):
        self.stat = sem("a_stat")
        self.var_done = sem("a_var_done")
        self.rstd_done = sem("a_rstd_done")
        self.zn_done = sem("a_zn_done")
        self.t_done = sem("a_t_done")
        self.zhi_done = sem("a_zhi_done")
        self.zlo_done = sem("a_zlo_done")
        self.q_done = sem("a_q_done")
        self.qhi_done = sem("a_qhi_done")
        self.qlo_done = sem("a_qlo_done")
        self.sc_done = sem("a_sc_done")
        self.max_done = sem("a_max_done")
        self.exp_done = sem("a_exp_done")
        self.tp_done = sem("a_tp_done")
        self.pT_done = sem("a_pT_done")
        self.u_done = sem("a_u_done")
        self.uT_done = sem("a_uT_done")
        self.out_done = sem("a_out_done")
        self.rinv_done = sem("a_rinv_done")
        self.fin_done = sem("a_fin_done")


def macaron_kernel(nc, x, Qw, Kw, Vw, Wg, bias_corr, W1, W2, Ws1, Ws2, out):
    B, S, D = x.shape
    E, I, _ = W1.shape
    NT = B * S // P
    TG = 4
    GT = TG * P
    NG = NT // TG
    F = E * I + Ws1.shape[0]
    NCH = F // P
    NC = E * I // P
    QT = S // P
    EG = E // N_GRP
    UN = 2
    AHEAD = 4
    HB = 3
    RING = 6
    WHOLE = (4, 5)
    PREP = 4
    PR = 4
    PADT = 3 * TG
    assert D == P and Ws1.shape[0] == P and NCH * UN % RING == 0 and NCH * UN % HB == 0 and NG % UN == 0 and PADT >= QT

    x_v = x.rearrange("b (t p) d -> p (b t) d", p=P)
    out_v = out.rearrange("b (t p) d -> p (b t) d", p=P)

    scratch = nc.dram_tensor("scratch", [2, NG, E, GT], F32, kind="Internal").ap()

    with ExitStack() as ctx:
        def sb(name, shape, dt=F32):
            return ctx.enter_context(nc.sbuf_tensor(name, shape, dt))

        def sem(name):
            return ctx.enter_context(nc.semaphore(name))

        x_sb = sb("x_sb", [P, NT + PADT, D])
        w_raw = sb("w_raw", [P, 2 * NCH * P])
        w1_raw = w_raw[:, 0:NCH * P].rearrange("p (c n) -> p c n", n=P)
        w2_raw = w_raw[:, NCH * P:].rearrange("p (c n) -> p c n", n=P)
        qk_raw = sb("qk_raw", [P, 2, D])
        wg_raw = sb("wg_raw", [E, D])
        w1_hi = sb("w1_hi", [P, NCH, P], F32R)
        w1_lo = sb("w1_lo", [P, NCH, P], F32R)
        w2_hi = sb("w2_hi", [P, NCH, D], F32R)
        w2_lo = sb("w2_lo", [P, NCH, D], F32R)
        w2_f = sb("w2_f", [P, len(WHOLE), D])
        wgT = sb("wgT", [P, E])
        qkT = sb("qkT", [P, 2, P])
        m_hi = sb("m_hi", [P, P], F32R)
        m_f = sb("m_f", [P, P])
        m_lo = sb("m_lo", [P, P], F32R)
        vw = sb("vw", [P, D])
        bias_bc = sb("bias_bc", [P, E])
        ident = sb("ident", [P, P])
        identb = sb("identb", [P, P], BF16)
        maskb = sb("maskb", [P, P], BF16)
        earlier = sb("earlier", [P, TG, N_GRP, N_GRP])
        tick = sb("tick", [P, 3])
        neg_half = sb("neg_half", [P, QT])
        bn = sb("bn", [P, QT, 6])
        mv = sb("mv", [P, QT, 2])
        rstd = sb("rstd", [P, QT])
        a_bn = sb("a_bn", [P, QT, 6])
        a_mv = sb("a_mv", [P, QT, 2])
        a_rstd = sb("a_rstd", [P, QT])
        shift = sb("shift", [P, TG])
        xn = sb("xn", [P, TG, D])
        x_f = sb("x_f", [P, UN, GT])
        x_hi = sb("x_hi", [P, UN, GT], F32R)
        x_lo = sb("x_lo", [P, UN, GT], F32R)
        scores = sb("scores", [P, UN, TG, E])
        inv = sb("inv", [P, TG, E])
        inv_u = sb("inv_u", [P, TG, E])
        inv_w = sb("inv_w", [P, TG, E])
        root = sb("root", [P, TG, E])
        choice = sb("choice", [P, TG, E])
        pair_hi = sb("pair_hi", [P, TG * N_GRP, 2])
        pair_lo = sb("pair_lo", [P, TG * N_GRP, 2])
        top1 = sb("top1", [P, TG * N_GRP])
        top2a = sb("top2a", [P, TG * N_GRP])
        top2b = sb("top2b", [P, TG * N_GRP])
        gscore = sb("gscore", [P, TG, N_GRP])
        beats = sb("beats", [P, TG, N_GRP, N_GRP])
        beats_eq = sb("beats_eq", [P, TG, N_GRP, N_GRP])
        grank = sb("grank", [P, TG, N_GRP])
        masked = sb("masked", [P, TG, E])
        cand = sb("cand", [P, TG, E + 4])
        top8 = sb("top8", [P, TG, 8])
        wanted = sb("wanted", [P, TG, 8])
        marked = sb("marked", [P, TG, E + 4])
        chosen = sb("chosen", [P, TG, E])
        wsum = sb("wsum", [P, TG])
        chosen_root = sb("chosen_root", [P, TG, E])
        wroot = sb("wroot", [P, TG])
        scw = sb("scw", [P, TG, E])
        wT = sb("wT", [E, GT])
        wb = sb("wb", [P, UN, NC, GT])
        s_sb = sb("s_sb", [P, RING, GT])
        shared = sb("shared", [P, PR * S])
        shared_r = sb("shared_r", [P, 2 * RING * GT], F32R)
        g_f = shared[:, 0:RING * GT].rearrange("p (r n) -> p r n", r=RING)
        g_hi = shared_r[:, 0:RING * GT].rearrange("p (r n) -> p r n", r=RING)
        g_lo = shared_r[:, RING * GT:].rearrange("p (r n) -> p r n", r=RING)
        oT = sb("oT", [P, GT])
        zn = sb("zn", [P, UN, QT, D])
        z_hi = sb("z_hi", [P, UN, S], F32R)
        z_lo = sb("z_lo", [P, UN, S], F32R)
        q_hi = [x_hi[:].rearrange("p u n -> p (u n)"), shared_r[:, 0:S]]
        q_lo = [x_lo[:].rearrange("p u n -> p (u n)"), shared_r[:, S:2 * S]]
        nmax = sb("nmax", [P, UN, QT])
        rsum = sb("rsum", [P, UN, QT])
        rinv = sb("rinv", [P, 2, QT // 2])
        prob = shared[:].rearrange("p (r n) -> p r n", r=PR)
        HQ = QT // 2
        pT = [w_raw[:, 0:HQ * HQ * P].rearrange("p (k q) -> p k q", k=HQ),
              wb[:, 1].rearrange("p c n -> p (c n)")[:, 0:QT * HQ * P].rearrange("p (k q) -> p k q", k=QT)]
        uT = s_sb[:, AHEAD:AHEAD + 2, :]

        psum = ctx.enter_context(nc.psum_tensor("psum", [P, 8, 512], F32))
        up_ps = [psum[:, b, :] for b in range(HB)]
        o_ps = [psum[:, 3, :], psum[:, 4, :]]
        tr_ps = psum[:, 5, :]
        lg_ps = psum[:, 6, :]
        wT_ps = psum[:, 7, :]
        sc_ps = [psum[:, 0:2, :].rearrange("p a n -> p (a n)"), psum[:, 2:4, :].rearrange("p a n -> p (a n)")]
        tp_ps = psum[:, 4:6, :].rearrange("p a n -> p (a n)")
        misc_ps = psum[:, 6, :]
        q_ps, z_ps = psum[:, 1, :], psum[:, 3, :]
        u_ps = psum[:, 7, :]

        x_in = [sem(f"x_in{g}") for g in range(4)]
        x_rest = sem("x_rest")
        w1_in, w2_in, small_in = sem("w1_in"), sem("w2_in"), sem("small_in")
        const_done, self_done = sem("const_done"), sem("const_self")
        wt_done, wt_hi, wt_free = sem("wt_done"), sem("wt_hi"), sem("wt_free")
        m_done, m_copied, m_hi_done, m_ready = sem("m_done"), sem("m_copied"), sem("m_hi_done"), sem("m_ready")
        stored = sem("stored")

        FF = [FfnSems(sem, "f0_"), FfnSems(sem, "f1_")]
        AT = AttentionSems(sem)

        def wait(eng, s, value):
            if not (isinstance(value, int) and value <= 0):
                eng.wait_ge(s, value)

        def nothing(step):
            pass

        block = ctx.enter_context(nc.Block())

        @block.sync
        def _(sp):
            for g in range(2):
                sp.dma_start(x_sb[:, TG * g:TG * (g + 1), :], x_v[:, TG * g:TG * (g + 1), :]).then_inc(x_in[g], 16)
            w1_rows = W1.rearrange("e i h -> (e i) h").rearrange("(c p) h -> p c h", p=P)
            sp.dma_start(w1_raw[:, 0:NC, :], w1_rows).then_inc(w1_in, 16)
            sp.dma_start(w1_raw[:, NC, :], Ws1).then_inc(w1_in, 16)
            for g in range(2, 4):
                sp.dma_start(x_sb[:, TG * g:TG * (g + 1), :], x_v[:, TG * g:TG * (g + 1), :]).then_inc(x_in[g], 16)
            sp.dma_start(x_sb[:, 4 * TG:NT, :], x_v[:, 4 * TG:NT, :]).then_inc(x_rest, 16)

            def ffn(phase):
                F = FF[phase]

                def spread(n, u):
                    sp.wait_ge(F.wT_done, n + 1)
                    row = scratch[phase, bass.ds(n, 1)].rearrange("n e t -> (n e) t")
                    sp.dma_start(row, wT[:]).then_inc(F.w_stored, 16)
                    sp.wait_ge(F.w_stored, 16 * (n + 1))
                    if phase == 1 and isinstance(n, int) and n < UN:
                        if n == 0:
                            sp.wait_ge(FF[0].s_done, NG * NCH)
                        else:
                            sp.wait_ge(AT.u_done, 2 * B)
                    if not (isinstance(n, int) and n < 2):
                        sp.wait_ge(F.s_done, NCH * (n - 1) + 1)
                    for e in range(P // I):
                        src = scratch[phase, bass.ds(n, 1)].rearrange("n (c e) t -> (n e) c t", e=P // I)[e:e + 1]
                        sp.dma_start(wb[e * I:(e + 1) * I, u], src.broadcast_to([I, NC, GT])).then_inc(F.w_loaded, 16)

                def store(g):
                    sp.wait_ge(F.res_done, g + 1)
                    sp.dma_start(out_v[:, bass.ds(g * TG, TG), :], x_sb[:, bass.ds(g * TG, TG), :]).then_inc(stored, 16)

                for n in range(2 * UN):
                    spread(n, n % UN)
                    if phase == 1 and n == 2 * UN - 1:
                        store(n - 3)
                with sp.Fori(2, NG // UN) as i:
                    for u in range(UN):
                        spread(i * UN + u, u)
                        if phase == 1:
                            store(i * UN + u - 3)
                if phase == 1:
                    for g in range(NG - 3, NG):
                        store(g)

            ffn(0)
            ffn(1)
            sp.wait_ge(stored, 16 * NG)

        @block.gpsimd
        def _(pool):
            nc.gpsimd.memset(ident[:], 0.0).then_inc(self_done, 1)
            nc.gpsimd.memset(maskb[:], 0.0).then_inc(self_done, 1)
            nc.gpsimd.memset(earlier[:], 1.0).then_inc(self_done, 1)
            nc.gpsimd.memset(neg_half[:], -0.5).then_inc(const_done, 1)
            pool.wait_ge(self_done, 3)
            nc.gpsimd.affine_select(out=ident[:], in_=ident[:], compare_op=ALU.not_equal, fill=1.0, base=0,
                                    pattern=[[-1, P]], channel_multiplier=1).then_inc(const_done, 1)
            nc.gpsimd.affine_select(out=maskb[:], in_=maskb[:], compare_op=ALU.is_ge, fill=MASKED, base=0,
                                    pattern=[[-1, P]], channel_multiplier=1).then_inc(const_done, 1)
            nc.gpsimd.affine_select(out=earlier[:], in_=earlier[:], compare_op=ALU.is_gt, fill=0.0, base=0,
                                    pattern=[[0, TG], [1, N_GRP], [-1, N_GRP]], channel_multiplier=0).then_inc(const_done, 1)
            nc.gpsimd.memset(x_sb[:, NT:NT + PADT, :], 0.0).then_inc(const_done, 1)

            def inv_std(S_, n, var, out_, readers):
                pool.wait_ge(S_.var_done, n + 1)
                for r, count in readers:
                    wait(pool, r, count)
                nc.gpsimd.tensor_tensor(out_, var, neg_half[:, 0:out_.shape[1]], ALU.pow).then_inc(S_.rstd_done, 1)

            def attention_inv(b):
                inv_std(AT, b, a_mv[:, :, 1], a_rstd[:], [(AT.zn_done, 2 * b)])

            def ffn(F):
                def norm_root(g):
                    pool.wait_ge(F.wsum_done, g + 1)
                    wait(pool, F.scw_done, g)
                    nc.gpsimd.tensor_tensor(wroot[:], wsum[:], neg_half[:, 0:TG], ALU.pow).then_inc(F.norm_done, 1)

                def lo_part(m, j):
                    if j % NCH in WHOLE:
                        return
                    pool.wait_ge(F.sq_done, m + 1)
                    nc.gpsimd.tensor_tensor(g_lo[:, j % RING, :], g_f[:, j % RING, :], g_hi[:, j % RING, :].bitcast(F32),
                                            ALU.subtract).then_inc(F.glo_done, 1)

                def x_lo_part(g, u):
                    pool.wait_ge(F.xhi_done, g + 1)
                    nc.gpsimd.tensor_tensor(x_lo[:, u, :], x_f[:, u, :], x_hi[:, u, :].bitcast(F32),
                                            ALU.subtract).then_inc(F.xlo_done, 1)

                def inv(n):
                    inv_std(F, n, mv[:, 0:TG, 1], rstd[:, 0:TG], [(F.xn_done, n), (F.xn2_done, n)])

                def start():
                    inv(0)
                    inv(1)
                    if F is FF[1]:
                        attention_inv(B - 1)
                    inv(2)
                    x_lo_part(0, 0)
                    norm_root(0)
                    x_lo_part(1, 1)
                    inv(3)
                    norm_root(1)
                    for m in range(AHEAD):
                        lo_part(m, m)

                def body(i, last):
                    for u in range(UN):
                        g = i * UN + u
                        for c in range(NCH):
                            j = u * NCH + c
                            if c == 0 and not last:
                                inv(g + PREP)
                            if c == 1 and not last:
                                norm_root(g + 2)
                            if c == 6 and not last:
                                x_lo_part(g + 2, u)
                            if last and F is FF[0] and j == 4:
                                attention_inv(0)
                            if not (last and j + AHEAD >= UN * NCH):
                                lo_part(i * (UN * NCH) + j + AHEAD, (j + AHEAD) % (UN * NCH))

                start()
                body(0, False)
                with pool.Fori(1, NG // UN - 1) as i:
                    body(i, False)
                body(NG // UN - 1, True)

            ffn(FF[0])
            with pool.Fori(1, B - 1) as b:
                attention_inv(b)
            ffn(FF[1])

        @block.scalar
        def _(sc):
            copy = lambda o, i, scale=1.0: nc.scalar.activation(o, i, ACT.Copy, scale=scale)

            sc.dma_start(w2_raw[:, 0:NC, :].rearrange("h c (j i) -> h (c j) i", i=I),
                         W2.rearrange("e h i -> h e i")).then_inc(w2_in, 16)
            sc.dma_start(w2_raw[:, NC, :], Ws2).then_inc(w2_in, 16)
            sc.dma_start(wg_raw[:], Wg).then_inc(small_in, 16)
            sc.dma_start(bias_bc[:], bias_corr.rearrange("(a e) -> a e", a=1).broadcast_to([P, E])).then_inc(small_in, 16)
            sc.dma_start(qk_raw[:, 0, :], Qw).then_inc(small_in, 16)
            sc.dma_start(qk_raw[:, 1, :], Kw).then_inc(small_in, 16)
            sc.dma_start(vw[:], Vw).then_inc(small_in, 16)

            def normalise(F, g, t):
                if t == 0:
                    sc.wait_ge(F.shift_done, g + 1)
                    wait(sc, F.xnT_done, g)
                ins = nc.scalar.activation(xn[:, t, :], x_sb[:, bass.ds(g * TG + t, 1), :].rearrange("p t d -> p (t d)"),
                                           ACT.Identity, bias=shift[:, t:t + 1], scale=rstd[:, t:t + 1])
                if t == TG // 2 - 1:
                    ins.then_inc(F.xn_done, 1)

            def ffn(F, phase):
                def x_copy(g, u, src):
                    sc.wait_ge(F.xnT_done, g + 1)
                    wait(sc, F.xlo_done, g - 1)
                    wait(sc, F.lg_done, g - 1)
                    copy(x_f[:, u, :], src).then_inc(F.xf_done, 1)

                def x_hi_copy(g, u):
                    sc.wait_ge(F.xf_done, g + 1)
                    wait(sc, F.up_done, NCH * (g - 1))
                    if phase == 1 and isinstance(g, int) and g < UN:
                        sc.wait_ge(AT.sc_done, QT * (B - 1))
                    copy(x_hi[:, u, :], x_f[:, u, :]).then_inc(F.xhi_done, 1)

                def sigmoid(g, u):
                    sc.wait_ge(F.lg_done, g + 1)
                    wait(sc, F.wsum_done, g - 1)
                    nc.scalar.activation(scores[:, u].rearrange("p t e -> p (t e)"), lg_ps[:, 0:TG * E],
                                         ACT.Sigmoid).then_inc(F.sig_done, 1)

                def wT_copy(g, src):
                    sc.wait_ge(F.scwT_done, g + 1)
                    wait(sc, F.w_stored, 16 * g)
                    copy(wT[:], src[0:E, :]).then_inc(F.wT_done, 1)

                def oT_copy(g, u):
                    sc.wait_ge(F.down_done, NCH * (g + 1))
                    wait(sc, F.oTr_done, g)
                    copy(oT[:], o_ps[u]).then_inc(F.oT_copied, 1)

                def square(m, j):
                    sc.wait_ge(F.s_done, m + 1)
                    wait(sc, F.down_done, m + 1 - RING)
                    if j % NCH not in WHOLE:
                        nc.scalar.activation(g_hi[:, j % RING, :], s_sb[:, j % RING, :], ACT.Square)
                    nc.scalar.activation(g_f[:, j % RING, :], s_sb[:, j % RING, :], ACT.Square).then_inc(F.sq_done, 1)

                def start(k):
                    for n in range(PREP):
                        if k == (1, 5, 9, 13)[n]:
                            for t in range(TG // 2):
                                normalise(F, n, t)
                        if k == (2, 7, 10, 14)[n]:
                            x_copy(n, n % UN, misc_ps)
                        if n < 3 and k == (4, 8, 11)[n]:
                            sigmoid(n, n % UN)
                        if n < 2 and k == (8, 9)[n]:
                            x_hi_copy(n, n)
                        if n < 2 and k == (12, 16)[n]:
                            wT_copy(n, (misc_ps, wT_ps)[n])

                def lead(c):
                    square(c, c)

                def body(i, first, last, extra):
                    for u in range(UN):
                        g = i * UN + u
                        for c in range(NCH):
                            j = u * NCH + c
                            if c == 0 and not (first and u == 0):
                                oT_copy(g - 1, 1 - u)
                            if c == 3 and not last:
                                sigmoid(g + 3, 1 - u)
                            if 4 <= c < 4 + TG // 2 and not last:
                                normalise(F, g + PREP, c - 4)
                            if c == 6 and not last:
                                x_hi_copy(g + 2, u)
                            if c == 7 and not last:
                                wT_copy(g + 2, wT_ps)
                            if c == 8 and not last:
                                x_copy(g + PREP, u, tr_ps)
                            if not (last and j + AHEAD >= UN * NCH):
                                square(i * (UN * NCH) + j + AHEAD, (j + AHEAD) % (UN * NCH))
                            extra(j)

                def run(extra):
                    body(0, True, False, nothing)
                    with sc.Fori(1, NG // UN - 1) as i:
                        body(i, False, False, nothing)
                    body(NG // UN - 1, False, True, extra)

                def close():
                    oT_copy(NG - 1, (NG - 1) % UN)

                return start, lead, run, close

            def attention(close_ffn, start_ffn, lead_ffn):
                A = AT

                def z_hi_copy(b, u, half, src):
                    sc.wait_ge(A.t_done, 2 * b + half + 1)
                    copy(z_hi[:, u, half * 512:half * 512 + 512], src).then_inc(A.zhi_done, 1)

                def q_hi_copy(b, u, half, src):
                    sc.wait_ge(A.q_done, 2 * b + half + 1)
                    copy(q_hi[u][:, half * 512:half * 512 + 512], src).then_inc(A.qhi_done, 1)

                def uT_copy(b, half):
                    sc.wait_ge(A.u_done, 2 * b + half + 1)
                    wait(sc, A.out_done, 2 * (b - 1) + half + 1)
                    copy(uT[:, half, :], u_ps).then_inc(A.uT_done, 1)

                def exp(b, t, u):
                    m = QT * b + t
                    sc.wait_ge(A.max_done, m + 1)
                    wait(sc, A.tp_done, m + 1 - PR)
                    w = (t + 1) * P
                    nc.scalar.activation(prob[:, t % PR, 0:w], sc_ps[t % 2][:, 0:w], ACT.Exp, bias=nmax[:, u, t:t + 1],
                                         accum_out=rsum[:, u, t:t + 1]).then_inc(A.exp_done, 1)

                def pT_copy(b, t):
                    m = QT * b + t
                    half, q0 = t // HQ, (t % HQ) * P
                    sc.wait_ge(A.tp_done, m + 1)
                    if t % HQ == 0:
                        wait(sc, A.u_done, 2 * (b - 1) + half + 1)
                    copy(pT[half][:, 0:t + 1, q0:q0 + P],
                         tp_ps[:, 0:(t + 1) * P].rearrange("p (k q) -> p k q", q=P)).then_inc(A.pT_done, 1)

                def begin(k):
                    if k == 10:
                        z_hi_copy(0, 0, 0, misc_ps)
                    if k == 13:
                        z_hi_copy(0, 0, 1, u_ps)
                    if k == 16:
                        q_hi_copy(0, 0, 0, misc_ps)

                def body(i, first, last):
                    for u in range(UN):
                        b = i * UN + u
                        old = not (first and u == 0)
                        new = not (last and u == UN - 1)
                        for t in range(QT):
                            if t == 0 and not old:
                                close_ffn()
                            if t == 4 and old:
                                uT_copy(b - 1, 1)
                            if t >= 2:
                                pT_copy(b, t - 2)
                            elif old:
                                pT_copy(b - 1, QT + t - 2)
                            exp(b, t, u)
                            if t == 0 and old:
                                uT_copy(b - 1, 0)
                                z_hi_copy(b, u, 1, z_ps)
                            if t == 2:
                                q_hi_copy(b, u, 1, q_ps)
                            if t == 6 and new:
                                z_hi_copy(b + 1, 1 - u, 0, misc_ps)
                            if t == 7 and new:
                                q_hi_copy(b + 1, 1 - u, 0, misc_ps)
                            if last:
                                start_ffn(u * QT + t)

                def run():
                    body(0, True, False)
                    with sc.Fori(1, B // UN - 1) as i:
                        body(i, False, False)
                    body(B // UN - 1, False, True)
                    pT_copy(B - 1, QT - 2)
                    uT_copy(B - 1, 0)
                    pT_copy(B - 1, QT - 1)
                    start_ffn(16)
                    for c in range(AHEAD - 1):
                        lead_ffn(c)
                    uT_copy(B - 1, 1)
                    lead_ffn(AHEAD - 1)

                return begin, run

            sc.wait_ge(const_done, 5)
            copy(identb[:], ident[:]).then_inc(m_copied, 1)
            start0, lead0, run0, close0 = ffn(FF[0], 0)
            start1, lead1, run1, close1 = ffn(FF[1], 1)
            start0(1)
            for w in range(5):
                sc.wait_ge(wt_done, w + 1)
                src = up_ps[w % 2]
                if w < 2:
                    copy(w1_hi[:, 4 * w:4 * w + 4, :].rearrange("p c n -> p (c n)"), src).then_inc(wt_hi, 1)
                elif w < 4:
                    for n, c in enumerate(WHOLE):
                        if 4 * (w - 2) <= c < 4 * (w - 1):
                            copy(w2_f[:, n, :], src[:, (c % 4) * P:(c % 4 + 1) * P])
                    copy(w2_hi[:, 4 * (w - 2):4 * (w - 2) + 4, :].rearrange("p c n -> p (c n)"), src).then_inc(wt_hi, 1)
                else:
                    copy(w1_hi[:, NC, :], src[:, 0:P])
                    copy(w2_hi[:, NC, :], src[:, P:2 * P])
                    copy(qkT[:].rearrange("p c n -> p (c n)"), src[:, 2 * P:4 * P]).then_inc(wt_hi, 1)
            sc.wait_ge(wt_done, 6)
            copy(wgT[:], up_ps[1][:, 0:E]).then_inc(wt_hi, 1)
            sc.wait_ge(m_done, 1)
            copy(m_f[:], up_ps[2][:, 0:P], scale=float(D) ** -0.5).then_inc(m_copied, 1)
            sc.wait_ge(m_copied, 2)
            copy(m_hi[:], m_f[:]).then_inc(m_hi_done, 1)

            for k in range(2, 17):
                start0(k)
            for c in range(AHEAD):
                lead0(c)
            begin_attention, run_attention = attention(close0, start1, lead1)
            run0(begin_attention)
            run_attention()
            run1(nothing)
            close1()

        @block.vector
        def _(v):
            tt = nc.vector.tensor_tensor
            f32 = lambda ap: ap.bitcast(F32)

            v.wait_ge(const_done, 5)
            nc.vector.memset(cand[:, :, E:E + 4], ABSENT).then_inc(FF[0].stat, 1)
            nc.vector.memset(wanted[:, :, 4:8], ABSENT).then_inc(FF[0].stat, 1)
            n_const = 2
            v.wait_ge(FF[0].stat, n_const)

            def lo_parts(w):
                v.wait_ge(wt_hi, w + 1)
                src = up_ps[w % 2]
                if w < 2:
                    cs = slice(4 * w, 4 * w + 4)
                    flat = lambda a: a[:, cs, :].rearrange("p c n -> p (c n)")
                    tt(flat(w1_lo), src, f32(flat(w1_hi)), ALU.subtract).then_inc(wt_free, 1)
                elif w < 4:
                    cs = slice(4 * (w - 2), 4 * (w - 2) + 4)
                    flat = lambda a: a[:, cs, :].rearrange("p c n -> p (c n)")
                    tt(flat(w2_lo), src, f32(flat(w2_hi)), ALU.subtract).then_inc(wt_free, 1)
                elif w == 4:
                    tt(w1_lo[:, NC, :], src[:, 0:P], f32(w1_hi[:, NC, :]), ALU.subtract)
                    tt(w2_lo[:, NC, :], src[:, P:2 * P], f32(w2_hi[:, NC, :]), ALU.subtract).then_inc(wt_free, 1)

            def carry(place):
                nc.vector.memset(tick[:, place:place + 1], 0.0)

            def norm_stats(S_, bn_, tile0, tiles):
                for t in tiles:
                    nc.vector.bn_stats(bn_[:, t, :], x_sb[:, bass.ds(tile0 + t, 1), :].rearrange("p t d -> p (t d)")).then_inc(S_.stat, 1)

            def norm_mean(S_, n, bn_, mv_, tiles, base):
                v.wait_ge(S_.stat, base + n * (2 * tiles) + tiles)
                carry(0)
                for t in range(tiles):
                    nc.vector.bn_aggr(mv_[:, t, :], bn_[:, t, :]).then_inc(S_.stat, 1)

            def norm_eps(S_, n, mv_, tiles, base):
                v.wait_ge(S_.stat, base + (n + 1) * (2 * tiles))
                nc.vector.tensor_scalar(mv_[:, 0:tiles, 1], mv_[:, 0:tiles, 1], LN_EPS, None, ALU.add).then_inc(S_.var_done, 1)

            def ffn(F, phase):
                base = n_const if phase == 0 else 0
                STEPS = (2, 7, 4, 6, 4, 6, 3, 4, 1, 0)
                N_ROUTE = sum(STEPS)

                def norm_shift(g):
                    v.wait_ge(F.rstd_done, g + 1)
                    wait(v, F.xn_done, g)
                    wait(v, F.xn2_done, g)
                    nc.vector.scalar_tensor_tensor(shift[:], mv[:, 0:TG, 0], -1.0, rstd[:, 0:TG],
                                                   ALU.mult, ALU.mult).then_inc(F.shift_done, 1)

                def stats(g, tiles):
                    norm_stats(F, bn, g * TG, tiles)

                def mean(g):
                    wait(v, F.shift_done, g)
                    norm_mean(F, g, bn, mv, TG, base)
                    norm_eps(F, g, mv, TG, base)

                def normalise(g, t):
                    v.wait_ge(F.shift_done, g + 1)
                    wait(v, F.xnT_done, g)
                    ins = nc.vector.tensor_scalar(xn[:, t, :], x_sb[:, bass.ds(g * TG + t, 1), :].rearrange("p t d -> p (t d)"),
                                                  rstd[:, t:t + 1], shift[:, t:t + 1], ALU.mult, ALU.add)
                    if t == TG - 1:
                        ins.then_inc(F.xn2_done, 1)

                def route(g, u, part):
                    done = [sum(STEPS[:part])]
                    score = scores[:, u]

                    def do(ins):
                        ins.then_inc(F.route, 1)
                        done[0] += 1

                    def after(k):
                        v.wait_ge(F.route, g * N_ROUTE + k)

                    def newton(part_):
                        if part_ == 0:
                            do(nc.vector.scalar_tensor_tensor(inv_u[:], inv[:], -0.5, score, ALU.mult, ALU.mult))
                        if part_ == 1:
                            do(tt(inv_w[:], inv_u[:], inv[:], ALU.mult))
                        if part_ == 2:
                            do(nc.vector.scalar_tensor_tensor(inv[:], inv_w[:], 1.5, inv[:], ALU.add, ALU.mult))

                    if part == 0:
                        v.wait_ge(F.sig_done, g + 1)
                        wait(v, F.wsum_done, g)
                        do(tt(choice[:], score, bias_bc[:].unsqueeze(1).to_broadcast([P, TG, E]), ALU.add))
                        do(nc.vector.tensor_scalar(inv[:].bitcast(I32), score.bitcast(I32), -0.5, float(RSQRT_GUESS),
                                                   ALU.mult, ALU.add))
                    if part == 1:
                        ch = choice[:].rearrange("p t (g e) -> p (t g) e", e=EG)
                        after(1)
                        do(tt(pair_hi[:], ch[:, :, 0:2], ch[:, :, 2:4], ALU.max))
                        do(tt(pair_lo[:], ch[:, :, 0:2], ch[:, :, 2:4], ALU.min))
                        after(2)
                        newton(0)
                        after(4)
                        do(tt(top2b[:], pair_lo[:, :, 0], pair_lo[:, :, 1], ALU.max))
                        do(tt(top2a[:], pair_hi[:, :, 0], pair_hi[:, :, 1], ALU.min))
                        do(tt(top1[:], pair_hi[:, :, 0], pair_hi[:, :, 1], ALU.max))
                        after(5)
                        newton(1)
                    if part == 2:
                        after(7)
                        do(tt(top2a[:], top2a[:], top2b[:], ALU.max))
                        after(9)
                        newton(2)
                        after(10)
                        do(tt(gscore[:].rearrange("p t g -> p (t g)"), top1[:], top2a[:], ALU.add))
                        after(11)
                        newton(0)
                    if part == 3:
                        gj = gscore[:].unsqueeze(2).to_broadcast([P, TG, N_GRP, N_GRP])
                        gg = gscore[:].unsqueeze(3).to_broadcast([P, TG, N_GRP, N_GRP])
                        after(12)
                        do(tt(beats_eq[:], gj, gg, ALU.is_equal))
                        do(tt(beats[:], gj, gg, ALU.is_gt))
                        after(14)
                        do(tt(beats_eq[:], beats_eq[:], earlier[:], ALU.mult))
                        after(13)
                        newton(1)
                        after(16)
                        do(tt(beats[:], beats[:], beats_eq[:], ALU.add))
                        after(17)
                        newton(2)
                    if part == 4:
                        after(18)
                        do(nc.vector.tensor_reduce(grank[:].rearrange("p t g -> p (t g)"),
                                                   beats[:].rearrange("p t g j -> p (t g) j"), AX.X, ALU.add))
                        after(19)
                        newton(0)
                        after(20)
                        do(nc.vector.scalar_tensor_tensor(
                            masked[:].rearrange("p t (g e) -> p (t g) e", e=EG),
                            grank[:].rearrange("p t g -> p (t g)").unsqueeze(2).to_broadcast([P, TG * N_GRP, EG]), TOPK_G - 0.5,
                            choice[:].rearrange("p t (g e) -> p (t g) e", e=EG), ALU.is_lt, ALU.mult))
                        after(21)
                        newton(1)
                    if part == 5:
                        after(22)
                        do(nc.vector.tensor_scalar(cand[:, :, 0:E], masked[:], 0.0, None, ALU.add))
                        after(23)
                        do(nc.vector.scalar_tensor_tensor(root[:], inv_w[:], 1.5, inv_u[:], ALU.add, ALU.mult))
                        after(24)
                        carry(1)
                        for t in range(TG):
                            do(nc.vector.max(top8[:, t, :], cand[:, t, 0:E]))
                    if part == 6:
                        after(29)
                        do(nc.vector.tensor_copy(wanted[:, :, 0:TOPK], top8[:, :, 0:TOPK]))
                        after(30)
                        carry(2)
                        for t in range(2):
                            do(nc.vector.match_replace(marked[:, t, :], wanted[:, t, :], cand[:, t, :], PICKED))
                    if part == 7:
                        for t in range(2, TG):
                            do(nc.vector.match_replace(marked[:, t, :], wanted[:, t, :], cand[:, t, :], PICKED))
                        after(34)
                        do(nc.vector.scalar_tensor_tensor(chosen[:], marked[:, :, 0:E], PICKED, score, ALU.is_ge, ALU.mult))
                        wait(v, F.scw_done, g)
                        do(nc.vector.scalar_tensor_tensor(chosen_root[:], marked[:, :, 0:E], PICKED, root[:], ALU.is_ge, ALU.mult))
                    if part == 8:
                        after(35)
                        do(nc.vector.tensor_reduce(wsum[:], chosen[:], AX.X, ALU.add))
                        after(37)
                        nc.vector.tensor_scalar(wsum[:], wsum[:], ROUTE_EPS, 1.0 / ROUTE_SCALE,
                                                ALU.add, ALU.mult).then_inc(F.wsum_done, 1)
                    if part == 9:
                        v.wait_ge(F.norm_done, g + 1)
                        wait(v, F.scwT_done, g)
                        nc.vector.scalar_tensor_tensor(scw[:], chosen_root[:], -2.0, wroot[:].unsqueeze(2).to_broadcast([P, TG, E]),
                                                       ALU.mult, ALU.mult).then_inc(F.scw_done, 1)
                    assert done[0] == sum(STEPS[:part + 1])

                def gate(g, c, m, j, u):
                    if c == 0:
                        v.wait_ge(F.w_loaded, 32 * (g + 1))
                    v.wait_ge(F.up_done, m + 1)
                    wait(v, F.sq_done, m + 1 - RING)
                    s_, h_ = s_sb[:, j % RING, :], up_ps[j % HB]
                    if c < NC:
                        ins = nc.vector.scalar_tensor_tensor(s_, h_, 0.0, wb[:, u, c, :], ALU.max, ALU.mult)
                    else:
                        ins = nc.vector.tensor_scalar(s_, h_, 0.0, None, ALU.max)
                    ins.then_inc(F.s_done, 1)

                def residual(g):
                    v.wait_ge(F.oTr_done, g + 1)
                    xs = x_sb[:, bass.ds(g * TG, TG), :].rearrange("p t d -> p (t d)")
                    nc.vector.scalar_tensor_tensor(xs, tr_ps, 0.5, xs, ALU.mult, ALU.add).then_inc(F.res_done, 1)

                def start(k):
                    for n in range(PREP + 1):
                        if k == (0, 2, 8, 12, 15)[n]:
                            if phase == 0:
                                v.wait_ge(x_in[n] if n < PREP else x_rest, 16)
                            elif n == 0:
                                v.wait_ge(AT.fin_done, 2 * (B - 3))
                            stats(n, range(TG))
                            if n < PREP:
                                mean(n)
                        if n < PREP and k == (1, 3, 9, 13)[n]:
                            norm_shift(n)
                            for t in range(TG // 2, TG):
                                normalise(n, t)
                    for n, slots in ((0, {5: (0, 1), 6: (2, 3), 7: (4, 5), 8: (6,), 9: (7, 8), 11: (9,)}),
                                     (1, {10: (0, 1), 11: (2, 3), 12: (4,), 13: (5, 6), 14: (7, 8), 16: (9,)}),
                                     (2, {17: (0, 1), 18: (2, 3), 19: (4, 5), 20: (6,)})):
                        for part in slots.get(k, ()):
                            route(n, n % UN, part)

                def lead(c):
                    gate(0, c, c, c, 0)
                    start(17 + c)

                def body(i, first, last, extra):
                    for u in range(UN):
                        g = i * UN + u
                        for c in range(NCH):
                            j = u * NCH + c
                            m = i * (UN * NCH) + j
                            if j + AHEAD < UN * NCH:
                                gate(g + (c + AHEAD) // NCH, (c + AHEAD) % NCH, m + AHEAD, j + AHEAD, (j + AHEAD) // NCH)
                            elif not last:
                                gate(g + 1, (c + AHEAD) % NCH, m + AHEAD, (j + AHEAD) % (UN * NCH), 0)
                            if not last:
                                if c == 0:
                                    mean(g + PREP)
                                if c == 1:
                                    stats(g + PREP + 1, range(2))
                                if c == 3:
                                    stats(g + PREP + 1, range(2, TG))
                                    norm_shift(g + PREP)
                                if 3 <= c < 3 + TG // 2:
                                    normalise(g + PREP, c - 3 + TG // 2)
                                for part in ((7,), (8,), (), (), (9,), (), (), (), ())[c]:
                                    route(g + 2, u, part)
                                for part in ((), (), (), (0,), (1,), (2,), (3,), (4,), (5, 6))[c]:
                                    route(g + 3, 1 - u, part)
                            if c == 2 and not (first and u == 0):
                                residual(g - 1)
                            extra(j)

                def run(extra):
                    if phase == 1:
                        v.wait_ge(AT.fin_done, 2 * B)
                    body(0, True, False, nothing)
                    with v.Fori(1, NG // UN - 1) as i:
                        body(i, False, False, nothing)
                    body(NG // UN - 1, False, True, extra)

                def close():
                    residual(NG - 1)

                return start, lead, run, close

            def attention(close_ffn, start_ffn, lead_ffn):
                A = AT

                def z_lo_part(b, u, half, src):
                    v.wait_ge(A.zhi_done, 2 * b + half + 1)
                    cs = slice(half * 512, half * 512 + 512)
                    tt(z_lo[:, u, cs], src, f32(z_hi[:, u, cs]), ALU.subtract).then_inc(A.zlo_done, 1)

                def q_lo_part(b, u, half, src):
                    v.wait_ge(A.qhi_done, 2 * b + half + 1)
                    cs = slice(half * 512, half * 512 + 512)
                    tt(q_lo[u][:, cs], src, f32(q_hi[u][:, cs]), ALU.subtract).then_inc(A.qlo_done, 1)

                def row_max(b, t, u):
                    v.wait_ge(A.sc_done, QT * b + t + 1)
                    nc.vector.tensor_reduce(nmax[:, u, t:t + 1], sc_ps[t % 2][:, 0:(t + 1) * P], AX.X, ALU.max,
                                            negate=True).then_inc(A.max_done, 1)

                def stats(b, half):
                    norm_stats(A, a_bn, b * QT, range(half * HQ, (half + 1) * HQ))

                def mean(b):
                    wait(v, A.zn_done, 2 * b)
                    norm_mean(A, b, a_bn, a_mv, QT, 0)

                def normalise(b, u, half):
                    v.wait_ge(A.rstd_done, b + 1)
                    wait(v, A.u_done, 2 * (b - 1))
                    for t in range(half * HQ, (half + 1) * HQ):
                        ins = nc.vector.tensor_scalar(zn[:, u, t, :], x_sb[:, bass.ds(b * QT + t, 1), :].rearrange("p t d -> p (t d)"),
                                                      a_mv[:, t, 0:1], a_rstd[:, t:t + 1], ALU.subtract, ALU.mult)
                    ins.then_inc(A.zn_done, 1)

                def finish(b, u, half):
                    v.wait_ge(A.exp_done, QT * b + (half + 1) * HQ)
                    nc.vector.reciprocal(rinv[:, half, :], rsum[:, u, half * HQ:(half + 1) * HQ]).then_inc(A.rinv_done, 1)
                    v.wait_ge(A.out_done, 2 * b + half + 1)
                    v.wait_ge(A.rinv_done, 2 * b + half + 1)
                    for t in range(HQ):
                        xs = x_sb[:, bass.ds(b * QT + half * HQ + t, 1), :].rearrange("p t d -> p (t d)")
                        ins = nc.vector.scalar_tensor_tensor(xs, misc_ps[:, t * P:(t + 1) * P], rinv[:, half, t:t + 1], xs,
                                                             ALU.mult, ALU.add)
                    ins.then_inc(A.fin_done, 1)

                def begin(k):
                    if k == 0:
                        v.wait_ge(FF[0].res_done, S // GT)
                        stats(0, 0)
                    if k == 1:
                        stats(0, 1)
                    if k == 2:
                        mean(0)
                    if k == 3:
                        norm_eps(A, 0, a_mv, QT, 0)
                    if k == 7:
                        normalise(0, 0, 0)
                    if k == 9:
                        normalise(0, 0, 1)
                    if k == 11:
                        z_lo_part(0, 0, 0, misc_ps)
                    if k == 14:
                        z_lo_part(0, 0, 1, u_ps)
                    if k == 17:
                        q_lo_part(0, 0, 0, misc_ps)

                def body(i, first, last):
                    for u in range(UN):
                        b = i * UN + u
                        old = not (first and u == 0)
                        new = not (last and u == UN - 1)
                        for t in range(QT):
                            if t == 6 and old:
                                finish(b - 1, 1 - u, 1)
                            row_max(b, t, u)
                            if t == 0 and not old:
                                close_ffn()
                                v.wait_ge(FF[0].res_done, NG)
                            if t < 2 and new:
                                stats(b + 1, t)
                            if t == 1 and old:
                                z_lo_part(b, u, 1, z_ps)
                            if t == 2 and old:
                                finish(b - 1, 1 - u, 0)
                            if t == 2 and new:
                                mean(b + 1)
                            if t == 3:
                                q_lo_part(b, u, 1, q_ps)
                            if t == 3 and new:
                                norm_eps(A, b + 1, a_mv, QT, 0)
                            if t == 5 and new:
                                normalise(b + 1, 1 - u, 0)
                            if t == 6 and new:
                                z_lo_part(b + 1, 1 - u, 0, misc_ps)
                                normalise(b + 1, 1 - u, 1)
                            if t == 7 and new:
                                q_lo_part(b + 1, 1 - u, 0, misc_ps)
                            if last:
                                start_ffn(u * QT + t)

                def run():
                    body(0, True, False)
                    with v.Fori(1, B // UN - 1) as i:
                        body(i, False, False)
                    body(B // UN - 1, False, True)
                    b, u = B - 1, (B - 1) % UN
                    start_ffn(16)
                    finish(b, u, 0)
                    for c in range(AHEAD - 1):
                        lead_ffn(c)
                    finish(b, u, 1)
                    lead_ffn(AHEAD - 1)

                return begin, run

            start0, lead0, run0, close0 = ffn(FF[0], 0)
            start1, lead1, run1, close1 = ffn(FF[1], 1)
            start0(0)
            start0(1)
            for w in range(5):
                lo_parts(w)
            v.wait_ge(m_hi_done, 1)
            tt(m_lo[:], m_f[:], f32(m_hi[:]), ALU.subtract).then_inc(m_ready, 1)
            v.wait_ge(small_in, 16 * 5)
            for k in range(2, 17):
                start0(k)
            for c in range(AHEAD):
                lead0(c)
            begin_attention, run_attention = attention(close0, start1, lead1)
            run0(begin_attention)
            run_attention()
            run1(nothing)
            close1()

        @block.tensor
        def _(pe):
            mm = nc.tensor.matmul

            def split3(out_, l_hi, l_lo, r_hi, r_lo, start=True, stop=True):
                mm(out_, l_hi, r_hi, start=start, stop=False)
                mm(out_, l_hi, r_lo, start=False, stop=False)
                return mm(out_, l_lo, r_hi, start=False, stop=stop)

            pe.wait_ge(const_done, 5)
            pe.wait_ge(w1_in, 32)
            for w in range(6):
                dst = up_ps[w % 2]
                if w == 2:
                    pe.wait_ge(w2_in, 32)
                if w == 4:
                    pe.wait_ge(small_in, 16 * 5)
                if w >= 2:
                    pe.wait_ge(wt_hi, w - 1)
                    pe.wait_ge(wt_free, w - 1)
                if w < 2:
                    srcs = [w1_raw[:, 4 * w + c, :] for c in range(4)]
                elif w < 4:
                    srcs = [w2_raw[:, 4 * (w - 2) + c, :] for c in range(4)]
                elif w == 4:
                    srcs = [w1_raw[:, NC, :], w2_raw[:, NC, :], qk_raw[:, 0, :], qk_raw[:, 1, :]]
                else:
                    srcs = []
                    nc.tensor.transpose(dst[:, 0:E], wg_raw[:], ident[0:E, 0:E]).then_inc(wt_done, 1)
                for c, src in enumerate(srcs):
                    ins = nc.tensor.transpose(dst[:, c * P:(c + 1) * P], src, ident[:])
                if srcs:
                    ins.then_inc(wt_done, 1)
            pe.wait_ge(wt_hi, 5)
            mm(up_ps[2][:, 0:P], qkT[:, 0, :], qkT[:, 1, :], start=True, stop=True).then_inc(m_done, 1)
            pe.wait_ge(wt_hi, 6)
            pe.wait_ge(wt_free, 5)
            pe.wait_ge(m_copied, 2)

            def ffn(F, phase):
                def xn_transpose(g, dst):
                    pe.wait_ge(F.xn_done, g + 1)
                    pe.wait_ge(F.xn2_done, g + 1)
                    for t in range(TG):
                        ins = nc.tensor.transpose(dst[:, t * P:(t + 1) * P], xn[:, t, :], ident[:])
                    ins.then_inc(F.xnT_done, 1)

                def logits(g, u):
                    pe.wait_ge(F.xf_done, g + 1)
                    wait(pe, F.sig_done, g)
                    for t in range(TG):
                        ins = mm(lg_ps[:, t * E:(t + 1) * E], x_f[:, u, t * P:(t + 1) * P], wgT[:], start=True, stop=True)
                    ins.then_inc(F.lg_done, 1)

                def w_transpose(g, dst):
                    pe.wait_ge(F.scw_done, g + 1)
                    wait(pe, F.wT_done, g)
                    for t in range(TG):
                        ins = nc.tensor.transpose(dst[0:E, t * P:(t + 1) * P], scw[:, t, :], ident[:])
                    ins.then_inc(F.scwT_done, 1)

                def up(g, c, m, j, u):
                    if c == 0:
                        pe.wait_ge(F.xlo_done, g + 1)
                    wait(pe, F.s_done, m + 1 - HB)
                    split3(up_ps[j % HB], w1_hi[:, c, :], w1_lo[:, c, :], x_hi[:, u, :], x_lo[:, u, :]).then_inc(F.up_done, 1)

                def down(g, c, m, j, u):
                    if c == 0:
                        wait(pe, F.oT_copied, g - 1)
                    if c in WHOLE:
                        pe.wait_ge(F.sq_done, m + 1)
                        mm(o_ps[u], w2_f[:, WHOLE.index(c), :], g_f[:, j % RING, :], start=(c == 0),
                           stop=(c == NCH - 1)).then_inc(F.down_done, 1)
                        return
                    pe.wait_ge(F.glo_done, g * (NCH - len(WHOLE)) + sum(k not in WHOLE for k in range(c + 1)))
                    split3(o_ps[u], w2_hi[:, c, :], w2_lo[:, c, :], g_hi[:, j % RING, :], g_lo[:, j % RING, :],
                           start=(c == 0), stop=(c == NCH - 1)).then_inc(F.down_done, 1)

                def o_transpose(g, copied):
                    pe.wait_ge(F.oT_copied, g + 1)
                    pe.wait_ge(F.xf_done, copied)
                    wait(pe, F.res_done, g)
                    for t in range(TG):
                        ins = nc.tensor.transpose(tr_ps[:, t * P:(t + 1) * P], oT[:, t * P:(t + 1) * P], ident[:])
                    ins.then_inc(F.oTr_done, 1)

                def start(k):
                    for n in range(PREP):
                        if k == (2, 7, 10, 14)[n]:
                            wait(pe, F.sig_done, n if n < 3 else 0)
                            if n == 3:
                                pe.wait_ge(F.wT_done, 1)
                            if phase == 1:
                                pe.wait_ge(*((AT.fin_done, 2 * (B - 3) + 1), (AT.qlo_done, 2 * (B - 1) + 1),
                                             (AT.fin_done, 2 * (B - 2) + 1), (AT.fin_done, 2 * (B - 1)))[n])
                            xn_transpose(n, misc_ps)
                        if n < 3 and k == (4, 8, 11)[n]:
                            logits(n, n % UN)
                    if k == 12:
                        pe.wait_ge(F.sig_done, 3)
                        w_transpose(0, misc_ps)
                    if k == 16:
                        w_transpose(1, wT_ps)

                def lead(c):
                    up(0, c, c, c, 0)

                def body(i, first, last, extra):
                    for u in range(UN):
                        g = i * UN + u
                        for c in range(NCH):
                            j = u * NCH + c
                            m = i * (UN * NCH) + j
                            if j + AHEAD < UN * NCH:
                                up(g + (c + AHEAD) // NCH, (c + AHEAD) % NCH, m + AHEAD, j + AHEAD, (j + AHEAD) // NCH)
                            elif not last:
                                up(g + 1, (c + AHEAD) % NCH, m + AHEAD, (j + AHEAD) % (UN * NCH), 0)
                            if c == 2 and not last:
                                logits(g + 3, 1 - u)
                            if c == 2 and not (first and u == 0):
                                o_transpose(g - 1, NG + 2 if last else g + PREP)
                            if c == 6 and not last:
                                w_transpose(g + 2, wT_ps)
                            if c == 7 and not last:
                                wait(pe, F.xf_done, g + PREP)
                                wait(pe, F.res_done, g)
                                xn_transpose(g + PREP, tr_ps)
                            down(g, c, m, j, u)
                            extra(j)

                def run(extra):
                    if phase == 1:
                        pe.wait_ge(AT.pT_done, QT * B)
                        pe.wait_ge(AT.fin_done, 2 * B)
                    body(0, True, False, nothing)
                    with pe.Fori(1, NG // UN - 1) as i:
                        body(i, False, False, nothing)
                    body(NG // UN - 1, False, True, extra)

                def close():
                    o_transpose(NG - 1, NG + 2)

                return start, lead, run, close

            def attention(close_ffn, start_ffn, lead_ffn):
                A = AT
                N1 = FF[1]

                def z_transpose(b, u, half, dst):
                    pe.wait_ge(A.zn_done, 2 * b + half + 1)
                    for t in range(HQ):
                        ins = nc.tensor.transpose(dst[:, t * P:(t + 1) * P], zn[:, u, half * HQ + t, :], ident[:])
                    ins.then_inc(A.t_done, 1)

                def q_product(b, u, half, dst):
                    pe.wait_ge(A.zlo_done, 2 * b + half + 1)
                    cs = slice(half * 512, half * 512 + 512)
                    split3(dst, m_hi[:], m_lo[:], z_hi[:, u, cs], z_lo[:, u, cs]).then_inc(A.q_done, 1)

                def score(b, t, u):
                    if t % HQ == 0:
                        pe.wait_ge(A.qlo_done, 2 * b + t // HQ + 1)
                    wait(pe, A.exp_done, QT * b + t - 1)
                    dst = sc_ps[t % 2]
                    w = (t + 1) * P
                    qs = slice(t * P, (t + 1) * P)
                    for c0 in range(0, w, 512):
                        c1 = min(c0 + 512, w)
                        ins = split3(dst[:, c0:c1], q_hi[u][:, qs], q_lo[u][:, qs], z_hi[:, u, c0:c1], z_lo[:, u, c0:c1],
                                     stop=(c1 < w))
                    mm(dst[:, t * P:w], identb[:], maskb[:], start=False, stop=True).then_inc(A.sc_done, 1)

                def prob_transpose(b, t):
                    m = QT * b + t
                    pe.wait_ge(A.exp_done, m + 1)
                    wait(pe, A.pT_done, m)
                    for k in range(t + 1):
                        ins = nc.tensor.transpose(tp_ps[:, k * P:(k + 1) * P], prob[:, t % PR, k * P:(k + 1) * P], ident[:])
                    ins.then_inc(A.tp_done, 1)

                def mix(b, u, half, k0, k1):
                    last = (half + 1) * HQ
                    if k0 == 0:
                        pe.wait_ge(A.pT_done, QT * b + last)
                        wait(pe, A.uT_done, 2 * b + half)
                    for k in range(k0, k1):
                        q0 = max(0, k - half * HQ) * P
                        ins = mm(u_ps[:, q0:], zn[:, u, k, :], pT[half][:, k, q0:], start=(k == 0), stop=(k == last - 1))
                    if k1 == last:
                        ins.then_inc(A.u_done, 1)

                def values(b, half):
                    pe.wait_ge(A.uT_done, 2 * b + half + 1)
                    if isinstance(b, int) and (b, half) in ((B - 3, 1), (B - 2, 0), (B - 2, 1), (B - 1, 0)):
                        pe.wait_ge(*{(B - 3, 1): (N1.sig_done, 1), (B - 2, 0): (N1.sig_done, 2), (B - 2, 1): (N1.wT_done, 1),
                                     (B - 1, 0): (N1.xf_done, PREP)}[b, half])
                    elif half == 0:
                        pe.wait_ge(A.qlo_done, 2 * b + 3)
                    else:
                        pe.wait_ge(A.fin_done, 2 * b + 1)
                    for t in range(HQ):
                        ins = mm(misc_ps[:, t * P:(t + 1) * P], uT[:, half, t * P:(t + 1) * P], vw[:], start=True, stop=True)
                    ins.then_inc(A.out_done, 1)

                def begin(k):
                    if k == 10:
                        z_transpose(0, 0, 0, misc_ps)
                    if k == 12:
                        z_transpose(0, 0, 1, u_ps)
                    if k == 15:
                        q_product(0, 0, 0, misc_ps)

                def body(i, first, last):
                    for u in range(UN):
                        b = i * UN + u
                        old = not (first and u == 0)
                        new = not (last and u == UN - 1)
                        for t in range(QT):
                            if t == 0 and old:
                                prob_transpose(b - 1, QT - 2)
                            score(b, t, u)
                            if t == 0 and not old:
                                close_ffn()
                            if t == 2 and not old:
                                pe.wait_ge(FF[0].res_done, NG)
                            if t >= 2:
                                prob_transpose(b, t - 2)
                            elif t == 1 and old:
                                prob_transpose(b - 1, QT - 1)
                            if t == 0 and old:
                                pe.wait_ge(A.exp_done, QT * b)
                                z_transpose(b, u, 1, z_ps)
                            if t == 1 and old:
                                values(b - 1, 0)
                            if t == 2:
                                pe.wait_ge(A.exp_done, QT * b + 1)
                                q_product(b, u, 1, q_ps)
                            if t == 2 and old:
                                mix(b - 1, 1 - u, 1, 0, HQ)
                            if t == 3 and old:
                                mix(b - 1, 1 - u, 1, HQ, QT)
                            if t == 5 and old:
                                values(b - 1, 1)
                            if t == 6 and new:
                                wait(pe, A.fin_done, 2 * b)
                                z_transpose(b + 1, 1 - u, 0, misc_ps)
                            if t == 7 and new:
                                q_product(b + 1, 1 - u, 0, misc_ps)
                            if t == 7:
                                mix(b, u, 0, 0, HQ)
                            if last:
                                start_ffn(u * QT + t)

                def run():
                    pe.wait_ge(m_ready, 1)
                    body(0, True, False)
                    with pe.Fori(1, B // UN - 1) as i:
                        body(i, False, False)
                    body(B // UN - 1, False, True)
                    b, u = B - 1, (B - 1) % UN
                    prob_transpose(b, QT - 2)
                    values(b, 0)
                    prob_transpose(b, QT - 1)
                    start_ffn(16)
                    pe.wait_ge(A.exp_done, QT * B)
                    for c in range(AHEAD - 1):
                        lead_ffn(c)
                    pe.wait_ge(N1.wT_done, UN)
                    mix(b, u, 1, 0, QT)
                    values(b, 1)
                    lead_ffn(AHEAD - 1)

                return begin, run

            start0, lead0, run0, close0 = ffn(FF[0], 0)
            start1, lead1, run1, close1 = ffn(FF[1], 1)
            for k in range(17):
                start0(k)
            for c in range(AHEAD):
                lead0(c)
            begin_attention, run_attention = attention(close0, start1, lead1)
            run0(begin_attention)
            run_attention()
            run1(nothing)
            close1()


_INS = ["L0_attn_x", "L0_attn_Qw", "L0_attn_Kw", "L0_attn_Vw", "L0_ffn_Wg", "L0_ffn_bias_corr", "L0_ffn_W1", "L0_ffn_W2",
        "L0_ffn_Ws1", "L0_ffn_Ws2"]


def kernel(**inputs):
    import numpy as _np
    import concourse.bacc as _bacc
    from concourse import mybir as _mybir
    from concourse.bass_utils import run_bass_kernel_spmd as _run

    nc = _bacc.Bacc("TRN2", target_bir_lowering=False, num_devices=1)
    arrays, args = {}, []
    for name in _INS:
        a = _np.ascontiguousarray(inputs[name])
        arrays[f"in_{name}"] = a
        args.append(nc.dram_tensor(f"in_{name}", a.shape, _mybir.dt.from_np(a.dtype), kind="ExternalInput").ap())
    shape = inputs["L0_attn_x"].shape
    args.append(nc.dram_tensor("out", shape, _mybir.dt.float32, kind="ExternalOutput").ap())
    macaron_kernel(nc, *args)
    r = _run(nc, [arrays], core_ids=[0])
    return r.results[0]["out"]
```

```python
from contextlib import ExitStack

import concourse.bass as bass
from concourse import mybir

F32 = mybir.dt.float32
F32R = mybir.dt.float32r
BF16 = mybir.dt.bfloat16
I32 = mybir.dt.int32
ALU = mybir.AluOpType
ACT = mybir.ActivationFunctionType
AX = mybir.AxisListType

P = 128
LN_EPS = 1e-5
TOPK_G = 2
TOPK = 4
N_GRP = 4
ROUTE_SCALE = 2.5
ROUTE_EPS = 1e-20
ABSENT = -3.0e38
PICKED = 3.4028234663852886e38
RSQRT_GUESS = 0x5f3759df
MASKED = -1.0e30


class FfnSems:
    def __init__(self, sem, tag):
        self.stat = sem(tag + "stat")
        self.var_done = sem(tag + "var_done")
        self.rstd_done = sem(tag + "rstd_done")
        self.shift_done = sem(tag + "shift_done")
        self.xn_done = sem(tag + "xn_done")
        self.xn2_done = sem(tag + "xn2_done")
        self.xnT_done = sem(tag + "xnT_done")
        self.xf_done = sem(tag + "xf_done")
        self.xhi_done = sem(tag + "xhi_done")
        self.xlo_done = sem(tag + "xlo_done")
        self.lg_done = sem(tag + "lg_done")
        self.sig_done = sem(tag + "sig_done")
        self.denom_done = sem(tag + "denom_done")
        self.score_done = sem(tag + "score_done")
        self.route = sem(tag + "route")
        self.wsum_done = sem(tag + "wsum_done")
        self.norm_done = sem(tag + "norm_done")
        self.scw_done = sem(tag + "scw_done")
        self.scwT_done = sem(tag + "scwT_done")
        self.wT_done = sem(tag + "wT_done")
        self.w_stored = sem(tag + "w_stored")
        self.w_loaded = sem(tag + "w_loaded")
        self.up_done = sem(tag + "up_done")
        self.s_done = sem(tag + "s_done")
        self.sq_done = sem(tag + "sq_done")
        self.glo_done = sem(tag + "glo_done")
        self.down_done = sem(tag + "down_done")
        self.oT_copied = sem(tag + "oT_copied")
        self.oTr_done = sem(tag + "oTr_done")
        self.res_done = sem(tag + "res_done")


class AttentionSems:
    def __init__(self, sem):
        self.stat = sem("a_stat")
        self.var_done = sem("a_var_done")
        self.rstd_done = sem("a_rstd_done")
        self.zn_done = sem("a_zn_done")
        self.t_done = sem("a_t_done")
        self.zhi_done = sem("a_zhi_done")
        self.zlo_done = sem("a_zlo_done")
        self.q_done = sem("a_q_done")
        self.qhi_done = sem("a_qhi_done")
        self.qlo_done = sem("a_qlo_done")
        self.sc_done = sem("a_sc_done")
        self.max_done = sem("a_max_done")
        self.exp_done = sem("a_exp_done")
        self.tp_done = sem("a_tp_done")
        self.pT_done = sem("a_pT_done")
        self.u_done = sem("a_u_done")
        self.uT_done = sem("a_uT_done")
        self.out_done = sem("a_out_done")
        self.rinv_done = sem("a_rinv_done")
        self.fin_done = sem("a_fin_done")


def macaron_kernel(nc, x, Qw, Kw, Vw, Wg, bias_corr, W1, W2, Ws1, Ws2, out):
    B, S, D = x.shape
    E, I, _ = W1.shape
    NT = B * S // P
    TG = 4
    GT = TG * P
    NG = NT // TG
    F = E * I + Ws1.shape[0]
    NCH = F // P
    NC = E * I // P
    QT = S // P
    EG = E // N_GRP
    UN = 2
    AHEAD = 4
    HB = 3
    RING = 6
    WHOLE = (1,)
    PREP = 4
    PR = 4
    PADT = 3 * TG
    assert D == P and Ws1.shape[0] == P and NCH * UN % RING == 0 and NCH * UN % HB == 0 and NG % UN == 0 and PADT >= QT >= 2 * TG

    x_v = x.rearrange("b (t p) d -> p (b t) d", p=P)
    out_v = out.rearrange("b (t p) d -> p (b t) d", p=P)

    scratch = nc.dram_tensor("scratch", [2, NG, E, GT], F32, kind="Internal").ap()

    with ExitStack() as ctx:
        def sb(name, shape, dt=F32):
            return ctx.enter_context(nc.sbuf_tensor(name, shape, dt))

        def sem(name):
            return ctx.enter_context(nc.semaphore(name))

        x_sb = sb("x_sb", [P, NT + PADT, D])
        w_raw = sb("w_raw", [P, 2 * NCH * P])
        w1_raw = w_raw[:, 0:NCH * P].rearrange("p (c n) -> p c n", n=P)
        w2_raw = w_raw[:, NCH * P:].rearrange("p (c n) -> p c n", n=P)
        qk_raw = sb("qk_raw", [P, 2, D])
        wg_raw = sb("wg_raw", [E, D])
        w1_hi = sb("w1_hi", [P, NCH, P], F32R)
        w1_lo = sb("w1_lo", [P, NCH, P], F32R)
        w2_hi = sb("w2_hi", [P, NCH, D], F32R)
        w2_lo = sb("w2_lo", [P, NCH, D], F32R)
        w2_f = sb("w2_f", [P, len(WHOLE), D])
        wgT = sb("wgT", [P, E])
        qkT = sb("qkT", [P, 2, P])
        m_hi = sb("m_hi", [P, P], F32R)
        m_f = sb("m_f", [P, P])
        m_lo = sb("m_lo", [P, P], F32R)
        vw = sb("vw", [P, D])
        bias_bc = sb("bias_bc", [P, E])
        ident = sb("ident", [P, P])
        identb = sb("identb", [P, P], BF16)
        maskb = sb("maskb", [P, P], BF16)
        earlier = sb("earlier", [P, TG, N_GRP, N_GRP])
        tick = sb("tick", [P, 3])
        neg_half = sb("neg_half", [P, QT])
        warm = sb("warm", [P, QT])
        bn = sb("bn", [P, QT, 6])
        mv = sb("mv", [P, QT, 2])
        powers = sb("powers", [P, 2 * TG])
        roots = sb("roots", [P, 2 * TG])
        var, wsum = powers[:, 0:TG], powers[:, TG:2 * TG]
        rstd, wroot = roots[:, 0:TG], roots[:, TG:2 * TG]
        a_bn = sb("a_bn", [P, QT, 6])
        a_mv = sb("a_mv", [P, QT, 2])
        a_rstd = sb("a_rstd", [P, QT])
        shift = sb("shift", [P, TG])
        xn = sb("xn", [P, TG, D])
        x_f = sb("x_f", [P, UN, GT])
        x_hi = sb("x_hi", [P, UN, GT], F32R)
        x_lo = sb("x_lo", [P, UN, GT], F32R)
        scores = sb("scores", [P, UN, TG, E])
        inv = sb("inv", [P, TG, E])
        inv_u = sb("inv_u", [P, TG, E])
        inv_w = sb("inv_w", [P, TG, E])
        root = sb("root", [P, TG, E])
        choice = sb("choice", [P, TG, E])
        pair_hi = sb("pair_hi", [P, TG * N_GRP, 2])
        pair_lo = sb("pair_lo", [P, TG * N_GRP, 2])
        top1 = sb("top1", [P, TG * N_GRP])
        top2a = sb("top2a", [P, TG * N_GRP])
        top2b = sb("top2b", [P, TG * N_GRP])
        gscore = sb("gscore", [P, TG, N_GRP])
        beats = sb("beats", [P, TG, N_GRP, N_GRP])
        beats_eq = sb("beats_eq", [P, TG, N_GRP, N_GRP])
        grank = sb("grank", [P, TG, N_GRP])
        masked = sb("masked", [P, TG, E])
        cand = sb("cand", [P, TG, E + 4])
        top8 = sb("top8", [P, TG, 8])
        wanted = sb("wanted", [P, TG, 8])
        marked = sb("marked", [P, TG, E + 4])
        chosen = sb("chosen", [P, TG, E])
        chosen_root = sb("chosen_root", [P, TG, E])
        scw = sb("scw", [P, P // TG, TG])
        wT = sb("wT", [E * TG, P])
        wb = sb("wb", [P, UN, NC, GT])
        s_sb = sb("s_sb", [P, RING, GT])
        shared = sb("shared", [P, PR * S])
        shared_r = sb("shared_r", [P, 2 * RING * GT], F32R)
        g_f = shared[:, 0:RING * GT].rearrange("p (r n) -> p r n", r=RING)
        g_hi = shared_r[:, 0:RING * GT].rearrange("p (r n) -> p r n", r=RING)
        g_lo = shared_r[:, RING * GT:].rearrange("p (r n) -> p r n", r=RING)
        oT = sb("oT", [P, GT])
        zn = sb("zn", [P, UN, QT, D])
        z_hi = sb("z_hi", [P, UN, S], F32R)
        z_lo = sb("z_lo", [P, UN, S], F32R)
        q_hi = [x_hi[:].rearrange("p u n -> p (u n)"), shared_r[:, 0:S]]
        q_lo = [x_lo[:].rearrange("p u n -> p (u n)"), shared_r[:, S:2 * S]]
        nmax = sb("nmax", [P, UN, QT])
        rsum = sb("rsum", [P, UN, QT])
        rinv = sb("rinv", [P, 2, QT // 2])
        prob = shared[:].rearrange("p (r n) -> p r n", r=PR)
        HQ = QT // 2
        pT = [w_raw[:, 0:HQ * HQ * P].rearrange("p (k q) -> p k q", k=HQ),
              wb[:, 1].rearrange("p c n -> p (c n)")[:, 0:QT * HQ * P].rearrange("p (k q) -> p k q", k=QT)]
        uT = s_sb[:, AHEAD:AHEAD + 2, :]

        psum = ctx.enter_context(nc.psum_tensor("psum", [P, 8, 512], F32))
        up_ps = [psum[:, b, :] for b in range(HB)]
        o_ps = [psum[:, 3, :], psum[:, 4, :]]
        tr_ps = psum[:, 5, :]
        lg_ps = psum[:, 6, :]
        wT_ps = psum[:, 7, :]
        sc_ps = [psum[:, 0:2, :].rearrange("p a n -> p (a n)"), psum[:, 2:4, :].rearrange("p a n -> p (a n)")]
        tp_ps = psum[:, 4:6, :].rearrange("p a n -> p (a n)")
        misc_ps = psum[:, 6, :]
        q_ps, z_ps = psum[:, 1, :], psum[:, 3, :]
        u_ps = psum[:, 7, :]
        wt_ps = [psum[:, b, :] for b in (0, 1, 3, 4, 2)]
        N_SETS = len(wt_ps)

        x_in = [sem(f"x_in{g}") for g in range(4)]
        x_rest = sem("x_rest")
        wg_in, bias_in, w1_in, w2_in, small_in = sem("wg_in"), sem("bias_in"), sem("w1_in"), sem("w2_in"), sem("small_in")
        const_done, self_done = sem("const_done"), sem("const_self")
        wgT_done, wgT_copied = sem("wgT_done"), sem("wgT_copied")
        wt_done, wt_hi, wt_lo = sem("wt_done"), sem("wt_hi"), sem("wt_lo")
        m_done, m_copied, m_hi_done, m_ready = sem("m_done"), sem("m_copied"), sem("m_hi_done"), sem("m_ready")
        stored = sem("stored")

        FF = [FfnSems(sem, "f0_"), FfnSems(sem, "f1_")]
        AT = AttentionSems(sem)

        def wait(eng, s, value):
            if not (isinstance(value, int) and value <= 0):
                eng.wait_ge(s, value)

        def nothing(step):
            pass

        block = ctx.enter_context(nc.Block())

        @block.sync
        def _(sp):
            sp.dma_start(x_sb[:, 0:TG, :], x_v[:, 0:TG, :]).then_inc(x_in[0], 16)
            sp.dma_start(wg_raw[:], Wg).then_inc(wg_in, 16)
            sp.dma_start(x_sb[:, TG:2 * TG, :], x_v[:, TG:2 * TG, :]).then_inc(x_in[1], 16)
            w1_rows = W1.rearrange("e i h -> (e i) h").rearrange("(c p) h -> p c h", p=P)
            sp.dma_start(w1_raw[:, 0:NC, :], w1_rows).then_inc(w1_in, 16)
            sp.dma_start(w1_raw[:, NC, :], Ws1).then_inc(w1_in, 16)
            sp.dma_start(bias_bc[:], bias_corr.rearrange("(a e) -> a e", a=1).broadcast_to([P, E])).then_inc(bias_in, 16)
            for g in range(2, 4):
                sp.dma_start(x_sb[:, TG * g:TG * (g + 1), :], x_v[:, TG * g:TG * (g + 1), :]).then_inc(x_in[g], 16)
            sp.dma_start(x_sb[:, 4 * TG:NT, :], x_v[:, 4 * TG:NT, :]).then_inc(x_rest, 16)
            sp.dma_start(qk_raw[:, 0, :], Qw).then_inc(small_in, 16)
            sp.dma_start(qk_raw[:, 1, :], Kw).then_inc(small_in, 16)
            sp.dma_start(vw[:], Vw).then_inc(small_in, 16)

            def ffn(phase):
                F = FF[phase]

                def spread(n, u):
                    sp.wait_ge(F.wT_done, n + 1)
                    row = scratch[phase, bass.ds(n, 1)].rearrange("n e (t p) -> (n e t) p", p=P)
                    sp.dma_start(row, wT[:]).then_inc(F.w_stored, 16)
                    sp.wait_ge(F.w_stored, 16 * (n + 1))
                    if phase == 1 and isinstance(n, int) and n < UN:
                        if n == 0:
                            sp.wait_ge(FF[0].s_done, NG * NCH)
                        else:
                            sp.wait_ge(AT.u_done, 2 * B)
                    if not (isinstance(n, int) and n < 2):
                        sp.wait_ge(F.s_done, NCH * (n - 1) + 1)
                    for e in range(P // I):
                        src = scratch[phase, bass.ds(n, 1)].rearrange("n (c e) t -> (n e) c t", e=P // I)[e:e + 1]
                        sp.dma_start(wb[e * I:(e + 1) * I, u], src.broadcast_to([I, NC, GT])).then_inc(F.w_loaded, 16)

                def store(g):
                    sp.wait_ge(F.res_done, g + 1)
                    sp.dma_start(out_v[:, bass.ds(g * TG, TG), :], x_sb[:, bass.ds(g * TG, TG), :]).then_inc(stored, 16)

                for n in range(2 * UN):
                    spread(n, n % UN)
                    if phase == 1 and n == 2 * UN - 1:
                        store(n - 3)
                with sp.Fori(2, NG // UN) as i:
                    for u in range(UN):
                        spread(i * UN + u, u)
                        if phase == 1:
                            store(i * UN + u - 3)
                if phase == 1:
                    for g in range(NG - 3, NG):
                        store(g)

            ffn(0)
            ffn(1)
            sp.wait_ge(stored, 16 * NG)

        @block.gpsimd
        def _(pool):
            nc.gpsimd.memset(ident[:], 0.0).then_inc(self_done, 1)
            nc.gpsimd.memset(maskb[:], 0.0).then_inc(self_done, 1)
            nc.gpsimd.memset(earlier[:], 1.0).then_inc(self_done, 1)
            nc.gpsimd.memset(neg_half[:], -0.5).then_inc(const_done, 1)
            pool.wait_ge(self_done, 3)
            nc.gpsimd.affine_select(out=ident[:], in_=ident[:], compare_op=ALU.not_equal, fill=1.0, base=0,
                                    pattern=[[-1, P]], channel_multiplier=1).then_inc(const_done, 1)
            nc.gpsimd.affine_select(out=maskb[:], in_=maskb[:], compare_op=ALU.is_ge, fill=MASKED, base=0,
                                    pattern=[[-1, P]], channel_multiplier=1).then_inc(const_done, 1)
            nc.gpsimd.affine_select(out=earlier[:], in_=earlier[:], compare_op=ALU.is_gt, fill=0.0, base=0,
                                    pattern=[[0, TG], [1, N_GRP], [-1, N_GRP]], channel_multiplier=0).then_inc(const_done, 1)
            nc.gpsimd.memset(x_sb[:, NT:NT + PADT, :], 0.0).then_inc(const_done, 1)

            def inv_std(S_, n, var, out_, readers):
                pool.wait_ge(S_.var_done, n + 1)
                for r, count in readers:
                    wait(pool, r, count)
                nc.gpsimd.tensor_tensor(out_, var, neg_half[:, 0:out_.shape[1]], ALU.pow).then_inc(S_.rstd_done, 1)

            def attention_inv(b):
                inv_std(AT, b, a_mv[:, :, 1], a_rstd[:], [(AT.zn_done, 2 * b)])

            def ffn(F):
                def norm_root(g):
                    pool.wait_ge(F.wsum_done, g + 1)
                    wait(pool, F.scw_done, g)
                    nc.gpsimd.tensor_tensor(wroot, wsum, neg_half[:, 0:TG], ALU.pow).then_inc(F.norm_done, 1)

                def lo_part(m, j):
                    if j % NCH in WHOLE:
                        return
                    pool.wait_ge(F.sq_done, m + 1)
                    nc.gpsimd.tensor_tensor(g_lo[:, j % RING, :], g_f[:, j % RING, :], g_hi[:, j % RING, :].bitcast(F32),
                                            ALU.subtract).then_inc(F.glo_done, 1)

                def x_lo_part(g, u):
                    pool.wait_ge(F.xhi_done, g + 1)
                    nc.gpsimd.tensor_tensor(x_lo[:, u, :], x_f[:, u, :], x_hi[:, u, :].bitcast(F32),
                                            ALU.subtract).then_inc(F.xlo_done, 1)

                def inv(n):
                    inv_std(F, n, var, rstd, [(F.xn_done, n), (F.xn2_done, n)])

                def inv_and_norm_root(g):
                    pool.wait_ge(F.var_done, g + PREP + 1)
                    pool.wait_ge(F.wsum_done, g + 3)
                    pool.wait_ge(F.xn_done, g + PREP)
                    pool.wait_ge(F.xn2_done, g + PREP)
                    pool.wait_ge(F.scw_done, g + 2)
                    nc.gpsimd.tensor_tensor(roots[:], powers[:], neg_half[:, 0:2 * TG], ALU.pow).then_inc(F.rstd_done, 1)

                def start():
                    inv(0)
                    inv(1)
                    if F is FF[0]:
                        x_lo_part(0, 0)
                        norm_root(0)
                        inv(2)
                    else:
                        attention_inv(B - 1)
                        inv(2)
                        x_lo_part(0, 0)
                        norm_root(0)
                    x_lo_part(1, 1)
                    inv(3)
                    norm_root(1)
                    for m in range(AHEAD):
                        lo_part(m, m)

                def body(i, last):
                    for u in range(UN):
                        g = i * UN + u
                        for c in range(NCH):
                            j = u * NCH + c
                            if c == 1 and not last:
                                inv_and_norm_root(g)
                            if c == 6 and not last:
                                x_lo_part(g + 2, u)
                            if last and F is FF[0] and j == 4:
                                attention_inv(0)
                            if not (last and j + AHEAD >= UN * NCH):
                                lo_part(i * (UN * NCH) + j + AHEAD, (j + AHEAD) % (UN * NCH))

                start()
                body(0, False)
                with pool.Fori(1, NG // UN - 1) as i:
                    body(i, False)
                body(NG // UN - 1, True)

            ffn(FF[0])
            with pool.Fori(1, B - 1) as b:
                attention_inv(b)
            ffn(FF[1])

        @block.scalar
        def _(sc):
            copy = lambda o, i, scale=1.0: nc.scalar.activation(o, i, ACT.Copy, scale=scale)

            sc.dma_start(w2_raw[:, 0:NC, :].rearrange("h c (j i) -> h (c j) i", i=I),
                         W2.rearrange("e h i -> h e i")).then_inc(w2_in, 16)
            sc.dma_start(w2_raw[:, NC, :], Ws2).then_inc(w2_in, 16)
            sc.wait_ge(const_done, 1)
            nc.scalar.activation(warm[:], neg_half[:], ACT.Sigmoid)

            def normalise(F, g, t):
                if t == 0:
                    sc.wait_ge(F.shift_done, g + 1)
                    wait(sc, F.xnT_done, g)
                ins = nc.scalar.activation(xn[:, t, :], x_sb[:, bass.ds(g * TG + t, 1), :].rearrange("p t d -> p (t d)"),
                                           ACT.Identity, bias=shift[:, t:t + 1], scale=rstd[:, t:t + 1])
                if t == TG // 2 - 1:
                    ins.then_inc(F.xn_done, 1)

            def ffn(F, phase):
                def x_copy(g, u, src):
                    sc.wait_ge(F.xnT_done, g + 1)
                    wait(sc, F.xlo_done, g - 1)
                    wait(sc, F.lg_done, g - 1)
                    copy(x_f[:, u, :], src).then_inc(F.xf_done, 1)

                def x_hi_copy(g, u):
                    sc.wait_ge(F.xf_done, g + 1)
                    wait(sc, F.up_done, NCH * (g - 1))
                    if phase == 1 and isinstance(g, int) and g < UN:
                        sc.wait_ge(AT.sc_done, QT * (B - 1))
                    copy(x_hi[:, u, :], x_f[:, u, :]).then_inc(F.xhi_done, 1)

                def sigmoid(g, u, src, by_exp=False):
                    sc.wait_ge(F.lg_done, g + 1)
                    wait(sc, F.wsum_done, g - 1)
                    nc.scalar.activation(scores[:, u].rearrange("p t e -> p (t e)"), src[:, 0:TG * E],
                                         ACT.Exp if by_exp else ACT.Sigmoid, scale=-1.0 if by_exp else 1.0).then_inc(F.sig_done, 1)

                def wT_copy(g, src):
                    sc.wait_ge(F.scwT_done, g + 1)
                    wait(sc, F.w_stored, 16 * g)
                    copy(wT[:], src[0:E * TG, 0:P]).then_inc(F.wT_done, 1)

                def oT_copy(g, u):
                    sc.wait_ge(F.down_done, NCH * (g + 1))
                    wait(sc, F.oTr_done, g)
                    copy(oT[:], o_ps[u]).then_inc(F.oT_copied, 1)

                def square(m, j):
                    sc.wait_ge(F.s_done, m + 1)
                    wait(sc, F.down_done, m + 1 - RING)
                    if j % NCH not in WHOLE:
                        nc.scalar.activation(g_hi[:, j % RING, :], s_sb[:, j % RING, :], ACT.Square)
                    nc.scalar.activation(g_f[:, j % RING, :], s_sb[:, j % RING, :], ACT.Square).then_inc(F.sq_done, 1)

                def first_half(n):
                    for t in range(TG // 2):
                        normalise(F, n, t)

                def opening():
                    first_half(0)
                    sc.wait_ge(wgT_done, 1)
                    copy(wgT[:], lg_ps[:, 0:E]).then_inc(wgT_copied, 1)
                    x_copy(0, 0, tr_ps)
                    sigmoid(0, 0, lg_ps)
                    first_half(1)
                    x_hi_copy(0, 0)
                    weights_hi(0)
                    x_copy(1, 1, tr_ps)
                    weights_hi(1)
                    sigmoid(1, 1, lg_ps)
                    weights_hi(2)
                    weights_hi(3)
                    x_hi_copy(1, 1)
                    wT_copy(0, wT_ps)
                    first_half(2)
                    x_copy(2, 0, tr_ps)
                    sigmoid(2, 0, lg_ps)
                    weights_hi(4)
                    first_half(3)
                    x_copy(3, 1, tr_ps)
                    attention_matrix()
                    lead(0)
                    wT_copy(1, wT_ps)
                    for c in range(1, AHEAD):
                        lead(c)

                def start(k):
                    for n in range(PREP):
                        if k == (1, 3, 9, 16)[n]:
                            first_half(n)
                        if k == (2, 4, 10, 17)[n]:
                            x_copy(n, n % UN, tr_ps)
                        if n < 3 and k == (3, 5, 11)[n]:
                            sigmoid(n, n % UN, tr_ps, by_exp=True)
                        if n < 2 and k == (8, 9)[n]:
                            x_hi_copy(n, n)
                        if n < 2 and k == (12, 16)[n]:
                            wT_copy(n, (tr_ps, wT_ps)[n])

                def lead(c):
                    square(c, c)

                def body(i, first, last, extra):
                    for u in range(UN):
                        g = i * UN + u
                        for c in range(NCH):
                            j = u * NCH + c
                            if c == 0 and not (first and u == 0):
                                oT_copy(g - 1, 1 - u)
                            if c == 3 and not last:
                                sigmoid(g + 3, 1 - u, lg_ps)
                            if 4 <= c < 4 + TG // 2 and not last:
                                normalise(F, g + PREP, c - 4)
                            if c == 6 and not last:
                                x_hi_copy(g + 2, u)
                            if c == 7 and not last:
                                wT_copy(g + 2, wT_ps)
                            if c == 8 and not last:
                                x_copy(g + PREP, u, tr_ps)
                            if not (last and j + AHEAD >= UN * NCH):
                                square(i * (UN * NCH) + j + AHEAD, (j + AHEAD) % (UN * NCH))
                            extra(j)

                def run(first_extra, last_extra):
                    body(0, True, False, first_extra)
                    with sc.Fori(1, NG // UN - 1) as i:
                        body(i, False, False, nothing)
                    body(NG // UN - 1, False, True, last_extra)

                def close():
                    oT_copy(NG - 1, (NG - 1) % UN)

                return opening, start, lead, run, close

            def attention(close_ffn, start_ffn, lead_ffn):
                A = AT

                def z_hi_copy(b, u, half, src):
                    sc.wait_ge(A.t_done, 2 * b + half + 1)
                    copy(z_hi[:, u, half * 512:half * 512 + 512], src).then_inc(A.zhi_done, 1)

                def q_hi_copy(b, u, half, src):
                    sc.wait_ge(A.q_done, 2 * b + half + 1)
                    copy(q_hi[u][:, half * 512:half * 512 + 512], src).then_inc(A.qhi_done, 1)

                def uT_copy(b, half):
                    sc.wait_ge(A.u_done, 2 * b + half + 1)
                    wait(sc, A.out_done, 2 * (b - 1) + half + 1)
                    copy(uT[:, half, :], u_ps).then_inc(A.uT_done, 1)

                def exp(b, t, u):
                    m = QT * b + t
                    sc.wait_ge(A.max_done, m + 1)
                    wait(sc, A.tp_done, m + 1 - PR)
                    w = (t + 1) * P
                    nc.scalar.activation(prob[:, t % PR, 0:w], sc_ps[t % 2][:, 0:w], ACT.Exp, bias=nmax[:, u, t:t + 1],
                                         accum_out=rsum[:, u, t:t + 1]).then_inc(A.exp_done, 1)

                def pT_copy(b, t):
                    m = QT * b + t
                    half, q0 = t // HQ, (t % HQ) * P
                    sc.wait_ge(A.tp_done, m + 1)
                    if t % HQ == 0:
                        wait(sc, A.u_done, 2 * (b - 1) + half + 1)
                    copy(pT[half][:, 0:t + 1, q0:q0 + P],
                         tp_ps[:, 0:(t + 1) * P].rearrange("p (k q) -> p k q", q=P)).then_inc(A.pT_done, 1)

                def begin(k):
                    if k == 10:
                        z_hi_copy(0, 0, 0, misc_ps)
                    if k == 13:
                        z_hi_copy(0, 0, 1, u_ps)
                    if k == 16:
                        q_hi_copy(0, 0, 0, misc_ps)

                def body(i, first, last):
                    for u in range(UN):
                        b = i * UN + u
                        old = not (first and u == 0)
                        new = not (last and u == UN - 1)
                        for t in range(QT):
                            if t == 0 and not old:
                                close_ffn()
                            if t >= 2:
                                pT_copy(b, t - 2)
                            elif old:
                                pT_copy(b - 1, QT + t - 2)
                            if t == 7 and new:
                                q_hi_copy(b + 1, 1 - u, 0, misc_ps)
                            exp(b, t, u)
                            if t == (3 if old else 2):
                                q_hi_copy(b, u, 1, q_ps)
                            if t == 3 and old:
                                uT_copy(b - 1, 1)
                            if t == 0 and old:
                                uT_copy(b - 1, 0)
                            if t == 1 and old:
                                z_hi_copy(b, u, 1, z_ps)
                            if t == 5 and new:
                                z_hi_copy(b + 1, 1 - u, 0, misc_ps)
                            if last:
                                start_ffn(u * QT + t)

                def run():
                    body(0, True, False)
                    with sc.Fori(1, B // UN - 1) as i:
                        body(i, False, False)
                    body(B // UN - 1, False, True)
                    uT_copy(B - 1, 0)
                    pT_copy(B - 1, QT - 2)
                    pT_copy(B - 1, QT - 1)
                    start_ffn(16)
                    for c in range(AHEAD - 1):
                        lead_ffn(c)
                    uT_copy(B - 1, 1)
                    start_ffn(17)
                    lead_ffn(AHEAD - 1)

                return begin, run

            def weights_hi(w):
                sc.wait_ge(wt_done, w + 1)
                src = wt_ps[w]
                flat = lambda a, k: a[:, 4 * k:4 * k + 4, :].rearrange("p c n -> p (c n)")
                if w < 2:
                    copy(flat(w1_hi, w), src).then_inc(wt_hi, 1)
                elif w < 4:
                    for n, c in enumerate(WHOLE):
                        if c // 4 == w - 2:
                            copy(w2_f[:, n, :], src[:, (c % 4) * P:(c % 4 + 1) * P])
                    copy(flat(w2_hi, w - 2), src).then_inc(wt_hi, 1)
                else:
                    copy(w1_hi[:, NC, :], src[:, 0:P])
                    copy(w2_hi[:, NC, :], src[:, P:2 * P])
                    copy(qkT[:].rearrange("p c n -> p (c n)"), src[:, 2 * P:4 * P]).then_inc(wt_hi, 1)

            def attention_matrix():
                copy(identb[:], ident[:]).then_inc(m_copied, 1)
                sc.wait_ge(m_done, 1)
                copy(m_f[:], o_ps[1][:, 0:P], scale=float(D) ** -0.5).then_inc(m_copied, 1)
                sc.wait_ge(m_copied, 2)
                copy(m_hi[:], m_f[:]).then_inc(m_hi_done, 1)

            sc.wait_ge(const_done, 5)
            opening0, _, _, run0, close0 = ffn(FF[0], 0)
            _, start1, lead1, run1, close1 = ffn(FF[1], 1)
            opening0()
            begin_attention, run_attention = attention(close0, start1, lead1)
            run0(nothing, begin_attention)
            run_attention()
            run1(nothing, nothing)
            close1()

        @block.vector
        def _(v):
            tt = nc.vector.tensor_tensor
            f32 = lambda ap: ap.bitcast(F32)

            v.wait_ge(const_done, 5)
            nc.vector.memset(cand[:, :, E:E + 4], ABSENT).then_inc(FF[0].stat, 1)
            nc.vector.memset(wanted[:, :, 4:8], ABSENT).then_inc(FF[0].stat, 1)
            nc.vector.memset(scw[:, E:, :], 0.0).then_inc(FF[0].stat, 1)
            n_const = 3
            v.wait_ge(FF[0].stat, n_const)

            def weights_lo(w):
                v.wait_ge(wt_hi, w + 1)
                src = wt_ps[w]
                flat = lambda a, k: a[:, 4 * k:4 * k + 4, :].rearrange("p c n -> p (c n)")
                if w < 2:
                    tt(flat(w1_lo, w), src, f32(flat(w1_hi, w)), ALU.subtract).then_inc(wt_lo, 1)
                elif w < 4:
                    tt(flat(w2_lo, w - 2), src, f32(flat(w2_hi, w - 2)), ALU.subtract).then_inc(wt_lo, 1)
                else:
                    tt(w1_lo[:, NC, :], src[:, 0:P], f32(w1_hi[:, NC, :]), ALU.subtract)
                    tt(w2_lo[:, NC, :], src[:, P:2 * P], f32(w2_hi[:, NC, :]), ALU.subtract).then_inc(wt_lo, 1)

            def carry(place):
                nc.vector.memset(tick[:, place:place + 1], 0.0)

            def norm_stats(S_, bn_, tile0, tiles):
                for t in tiles:
                    nc.vector.bn_stats(bn_[:, t, :], x_sb[:, bass.ds(tile0 + t, 1), :].rearrange("p t d -> p (t d)")).then_inc(S_.stat, 1)

            def norm_mean(S_, n, bn_, mv_, tiles, base):
                v.wait_ge(S_.stat, base + n * (2 * tiles) + tiles)
                carry(0)
                for t in range(tiles):
                    nc.vector.bn_aggr(mv_[:, t, :], bn_[:, t, :]).then_inc(S_.stat, 1)

            def norm_eps(S_, n, mv_, tiles, base, out_):
                v.wait_ge(S_.stat, base + (n + 1) * (2 * tiles))
                nc.vector.tensor_scalar(out_, mv_[:, 0:tiles, 1], LN_EPS, None, ALU.add).then_inc(S_.var_done, 1)

            def ffn(F, phase):
                base = n_const if phase == 0 else 0
                STEPS = (2, 7, 4, 6, 4, 6, 3, 4, 1, 0)
                N_ROUTE = sum(STEPS)

                def norm_shift(g):
                    v.wait_ge(F.rstd_done, g + 1)
                    wait(v, F.xn_done, g)
                    wait(v, F.xn2_done, g)
                    nc.vector.scalar_tensor_tensor(shift[:], mv[:, 0:TG, 0], -1.0, rstd[:, 0:TG],
                                                   ALU.mult, ALU.mult).then_inc(F.shift_done, 1)

                def stats(g, tiles):
                    norm_stats(F, bn, g * TG, tiles)

                def mean(g):
                    wait(v, F.shift_done, g)
                    norm_mean(F, g, bn, mv, TG, base)
                    norm_eps(F, g, mv, TG, base, var)

                def normalise(g, t):
                    v.wait_ge(F.shift_done, g + 1)
                    wait(v, F.xnT_done, g)
                    ins = nc.vector.tensor_scalar(xn[:, t, :], x_sb[:, bass.ds(g * TG + t, 1), :].rearrange("p t d -> p (t d)"),
                                                  rstd[:, t:t + 1], shift[:, t:t + 1], ALU.mult, ALU.add)
                    if t == TG - 1:
                        ins.then_inc(F.xn2_done, 1)

                def route(g, u, part):
                    done = [sum(STEPS[:part])]
                    score = scores[:, u]

                    def do(ins):
                        ins.then_inc(F.route, 1)
                        done[0] += 1

                    def after(k):
                        v.wait_ge(F.route, g * N_ROUTE + k)

                    def newton(part_):
                        if part_ == 0:
                            do(nc.vector.scalar_tensor_tensor(inv_u[:], inv[:], -0.5, score, ALU.mult, ALU.mult))
                        if part_ == 1:
                            do(tt(inv_w[:], inv_u[:], inv[:], ALU.mult))
                        if part_ == 2:
                            do(nc.vector.scalar_tensor_tensor(inv[:], inv_w[:], 1.5, inv[:], ALU.add, ALU.mult))

                    if part == 0:
                        v.wait_ge(F.sig_done, g + 1)
                        if phase == 1 and isinstance(g, int) and g < 3:
                            nc.vector.tensor_scalar(score, score, 1.0, None, ALU.add).then_inc(F.denom_done, 1)
                            v.wait_ge(F.denom_done, g + 1)
                            nc.vector.reciprocal(score, score).then_inc(F.score_done, 1)
                            v.wait_ge(F.score_done, g + 1)
                        wait(v, F.wsum_done, g)
                        do(tt(choice[:], score, bias_bc[:].unsqueeze(1).to_broadcast([P, TG, E]), ALU.add))
                        do(nc.vector.tensor_scalar(inv[:].bitcast(I32), score.bitcast(I32), -0.5, float(RSQRT_GUESS),
                                                   ALU.mult, ALU.add))
                    if part == 1:
                        ch = choice[:].rearrange("p t (g e) -> p (t g) e", e=EG)
                        after(1)
                        do(tt(pair_hi[:], ch[:, :, 0:2], ch[:, :, 2:4], ALU.max))
                        do(tt(pair_lo[:], ch[:, :, 0:2], ch[:, :, 2:4], ALU.min))
                        after(2)
                        newton(0)
                        after(4)
                        do(tt(top2b[:], pair_lo[:, :, 0], pair_lo[:, :, 1], ALU.max))
                        do(tt(top2a[:], pair_hi[:, :, 0], pair_hi[:, :, 1], ALU.min))
                        do(tt(top1[:], pair_hi[:, :, 0], pair_hi[:, :, 1], ALU.max))
                        after(5)
                        newton(1)
                    if part == 2:
                        after(7)
                        do(tt(top2a[:], top2a[:], top2b[:], ALU.max))
                        after(9)
                        newton(2)
                        after(10)
                        do(tt(gscore[:].rearrange("p t g -> p (t g)"), top1[:], top2a[:], ALU.add))
                        after(11)
                        newton(0)
                    if part == 3:
                        gj = gscore[:].unsqueeze(2).to_broadcast([P, TG, N_GRP, N_GRP])
                        gg = gscore[:].unsqueeze(3).to_broadcast([P, TG, N_GRP, N_GRP])
                        after(12)
                        do(tt(beats_eq[:], gj, gg, ALU.is_equal))
                        do(tt(beats[:], gj, gg, ALU.is_gt))
                        after(14)
                        do(tt(beats_eq[:], beats_eq[:], earlier[:], ALU.mult))
                        after(13)
                        newton(1)
                        after(16)
                        do(tt(beats[:], beats[:], beats_eq[:], ALU.add))
                        after(17)
                        newton(2)
                    if part == 4:
                        after(18)
                        do(nc.vector.tensor_reduce(grank[:].rearrange("p t g -> p (t g)"),
                                                   beats[:].rearrange("p t g j -> p (t g) j"), AX.X, ALU.add))
                        after(19)
                        newton(0)
                        after(20)
                        do(nc.vector.scalar_tensor_tensor(
                            masked[:].rearrange("p t (g e) -> p (t g) e", e=EG),
                            grank[:].rearrange("p t g -> p (t g)").unsqueeze(2).to_broadcast([P, TG * N_GRP, EG]), TOPK_G - 0.5,
                            choice[:].rearrange("p t (g e) -> p (t g) e", e=EG), ALU.is_lt, ALU.mult))
                        after(21)
                        newton(1)
                    if part == 5:
                        after(22)
                        do(nc.vector.tensor_scalar(cand[:, :, 0:E], masked[:], 0.0, None, ALU.add))
                        after(23)
                        do(nc.vector.scalar_tensor_tensor(root[:], inv_w[:], 1.5, inv_u[:], ALU.add, ALU.mult))
                        after(24)
                        carry(1)
                        for t in range(TG):
                            do(nc.vector.max(top8[:, t, :], cand[:, t, 0:E]))
                    if part == 6:
                        after(29)
                        do(nc.vector.tensor_copy(wanted[:, :, 0:TOPK], top8[:, :, 0:TOPK]))
                        after(30)
                        carry(2)
                        for t in range(2):
                            do(nc.vector.match_replace(marked[:, t, :], wanted[:, t, :], cand[:, t, :], PICKED))
                    if part == 7:
                        for t in range(2, TG):
                            do(nc.vector.match_replace(marked[:, t, :], wanted[:, t, :], cand[:, t, :], PICKED))
                        after(34)
                        do(nc.vector.scalar_tensor_tensor(chosen[:], marked[:, :, 0:E], PICKED, score, ALU.is_ge, ALU.mult))
                        wait(v, F.scw_done, g)
                        do(nc.vector.scalar_tensor_tensor(chosen_root[:], marked[:, :, 0:E], PICKED, root[:], ALU.is_ge, ALU.mult))
                    if part == 8:
                        after(35)
                        do(nc.vector.tensor_reduce(wsum, chosen[:], AX.X, ALU.add))
                        after(37)
                        nc.vector.tensor_scalar(wsum, wsum, ROUTE_EPS, 1.0 / ROUTE_SCALE,
                                                ALU.add, ALU.mult).then_inc(F.wsum_done, 1)
                    if part == 9:
                        if isinstance(g, int) and g < 2:
                            v.wait_ge(F.norm_done, g + 1)
                        else:
                            v.wait_ge(F.rstd_done, g + PREP - 1)
                        wait(v, F.scwT_done, g)
                        nc.vector.scalar_tensor_tensor(scw[:, 0:E, :].rearrange("p e t -> p t e"), chosen_root[:], -2.0, wroot.unsqueeze(2).to_broadcast([P, TG, E]),
                                                       ALU.mult, ALU.mult).then_inc(F.scw_done, 1)
                    assert done[0] == sum(STEPS[:part + 1])

                def gate(g, c, m, j, u):
                    if c == 0:
                        v.wait_ge(F.w_loaded, 32 * (g + 1))
                    v.wait_ge(F.up_done, m + 1)
                    wait(v, F.sq_done, m + 1 - RING)
                    s_, h_ = s_sb[:, j % RING, :], up_ps[j % HB]
                    if c < NC:
                        ins = nc.vector.scalar_tensor_tensor(s_, h_, 0.0, wb[:, u, c, :], ALU.max, ALU.mult)
                    else:
                        ins = nc.vector.tensor_scalar(s_, h_, 0.0, None, ALU.max)
                    ins.then_inc(F.s_done, 1)

                def residual(g):
                    v.wait_ge(F.oTr_done, g + 1)
                    xs = x_sb[:, bass.ds(g * TG, TG), :].rearrange("p t d -> p (t d)")
                    nc.vector.scalar_tensor_tensor(xs, tr_ps, 0.5, xs, ALU.mult, ALU.add).then_inc(F.res_done, 1)

                def second_half(n):
                    norm_shift(n)
                    for t in range(TG // 2, TG):
                        normalise(n, t)

                def route_parts(n, *parts):
                    for part in parts:
                        route(n, n % UN, part)

                def opening():
                    def statistics(n):
                        v.wait_ge(x_in[n], 16)
                        stats(n, range(TG))
                        mean(n)

                    statistics(0)
                    second_half(0)
                    statistics(1)
                    second_half(1)
                    v.wait_ge(bias_in, 16)
                    route_parts(0, 0, 1, 2, 3, 4, 5, 6, 7, 8)
                    statistics(2)
                    route_parts(0, 9)
                    weights_lo(0)
                    weights_lo(1)
                    second_half(2)
                    statistics(3)
                    route_parts(1, 0, 1)
                    weights_lo(2)
                    weights_lo(3)
                    second_half(3)
                    route_parts(1, 2)
                    weights_lo(4)
                    route_parts(1, 3, 4, 5, 6, 7, 8)
                    v.wait_ge(x_rest, 16)
                    for c in range(AHEAD):
                        lead(c)

                def start(k):
                    for n in range(PREP + 1):
                        if k == (0, 2, 8, 14, 16 if phase == 1 else 18)[n]:
                            if n == 0:
                                v.wait_ge(AT.fin_done, 2 * (B - 3))
                            stats(n, range(TG))
                            if n < PREP:
                                mean(n)
                        if n < PREP and k == (1, 3, 9, 15)[n]:
                            second_half(n)
                    for n, slots in ((0, {6: (0, 1), 7: (2, 3), 8: (4, 5, 6), 9: (7, 8), 10: (9,)}),
                                     (1, {10: (0,), 11: (1, 2), 12: (3,), 13: (4, 5), 14: (6,), 15: (7, 8), 16 if phase == 1 else 17: (9,)}),
                                     (2, {16: (0, 1), 17: (2, 3), 18: (4, 5), 19: (6,)} if phase == 1 else
                                         {18: (0, 1), 19: (2, 3), 20: (4, 5, 6)})):
                        route_parts(n, *slots.get(k, ()))
                    if phase == 0 and k == 17:
                        v.wait_ge(m_hi_done, 1)
                        tt(m_lo[:], m_f[:], f32(m_hi[:]), ALU.subtract).then_inc(m_ready, 1)

                def lead(c):
                    gate(0, c, c, c, 0)
                    start(17 + c)

                def body(i, first, last, extra):
                    for u in range(UN):
                        g = i * UN + u
                        for c in range(NCH):
                            j = u * NCH + c
                            m = i * (UN * NCH) + j
                            if j + AHEAD < UN * NCH:
                                gate(g + (c + AHEAD) // NCH, (c + AHEAD) % NCH, m + AHEAD, j + AHEAD, (j + AHEAD) // NCH)
                            elif not last:
                                gate(g + 1, (c + AHEAD) % NCH, m + AHEAD, (j + AHEAD) % (UN * NCH), 0)
                            if not last:
                                if c == 0:
                                    mean(g + PREP)
                                if c == 1:
                                    stats(g + PREP + 1, range(2))
                                if c == 3:
                                    stats(g + PREP + 1, range(2, TG))
                                    norm_shift(g + PREP)
                                if 3 <= c < 3 + TG // 2:
                                    normalise(g + PREP, c - 3 + TG // 2)
                                for part in ((7,), (8,), (), (), (9,), (), (), (), ())[c]:
                                    route(g + 2, u, part)
                                for part in ((), (), (), (0,), (1,), (2,), (3,), (4,), (5, 6))[c]:
                                    route(g + 3, 1 - u, part)
                            if c == 2 and not (first and u == 0):
                                residual(g - 1)
                            extra(j)

                def run(first_extra, last_extra):
                    body(0, True, False, first_extra)
                    if phase == 1:
                        v.wait_ge(AT.fin_done, 2 * B)
                    with v.Fori(1, NG // UN - 1) as i:
                        body(i, False, False, nothing)
                    body(NG // UN - 1, False, True, last_extra)

                def close():
                    residual(NG - 1)

                return opening, start, lead, run, close

            def attention(close_ffn, start_ffn, lead_ffn):
                A = AT

                def z_lo_part(b, u, half, src):
                    v.wait_ge(A.zhi_done, 2 * b + half + 1)
                    cs = slice(half * 512, half * 512 + 512)
                    tt(z_lo[:, u, cs], src, f32(z_hi[:, u, cs]), ALU.subtract).then_inc(A.zlo_done, 1)

                def q_lo_part(b, u, half, src):
                    v.wait_ge(A.qhi_done, 2 * b + half + 1)
                    cs = slice(half * 512, half * 512 + 512)
                    tt(q_lo[u][:, cs], src, f32(q_hi[u][:, cs]), ALU.subtract).then_inc(A.qlo_done, 1)

                def row_max(b, t, u):
                    v.wait_ge(A.sc_done, QT * b + t + 1)
                    nc.vector.tensor_reduce(nmax[:, u, t:t + 1], sc_ps[t % 2][:, 0:(t + 1) * P], AX.X, ALU.max,
                                            negate=True).then_inc(A.max_done, 1)

                def stats(b, half):
                    norm_stats(A, a_bn, b * QT, range(half * HQ, (half + 1) * HQ))

                def mean(b):
                    wait(v, A.zn_done, 2 * b)
                    norm_mean(A, b, a_bn, a_mv, QT, 0)

                def normalise(b, u, half):
                    v.wait_ge(A.rstd_done, b + 1)
                    wait(v, A.u_done, 2 * (b - 1))
                    for t in range(half * HQ, (half + 1) * HQ):
                        ins = nc.vector.tensor_scalar(zn[:, u, t, :], x_sb[:, bass.ds(b * QT + t, 1), :].rearrange("p t d -> p (t d)"),
                                                      a_mv[:, t, 0:1], a_rstd[:, t:t + 1], ALU.subtract, ALU.mult)
                    ins.then_inc(A.zn_done, 1)

                def finish(b, u, half):
                    v.wait_ge(A.exp_done, QT * b + (half + 1) * HQ)
                    nc.vector.reciprocal(rinv[:, half, :], rsum[:, u, half * HQ:(half + 1) * HQ]).then_inc(A.rinv_done, 1)
                    v.wait_ge(A.out_done, 2 * b + half + 1)
                    v.wait_ge(A.rinv_done, 2 * b + half + 1)
                    for t in range(HQ):
                        xs = x_sb[:, bass.ds(b * QT + half * HQ + t, 1), :].rearrange("p t d -> p (t d)")
                        ins = nc.vector.scalar_tensor_tensor(xs, misc_ps[:, t * P:(t + 1) * P], rinv[:, half, t:t + 1], xs,
                                                             ALU.mult, ALU.add)
                    ins.then_inc(A.fin_done, 1)

                def begin(k):
                    if k == 0:
                        v.wait_ge(FF[0].res_done, S // GT)
                        stats(0, 0)
                    if k == 1:
                        stats(0, 1)
                    if k == 2:
                        mean(0)
                    if k == 3:
                        norm_eps(A, 0, a_mv, QT, 0, a_mv[:, :, 1])
                    if k == 7:
                        normalise(0, 0, 0)
                    if k == 9:
                        normalise(0, 0, 1)
                    if k == 11:
                        z_lo_part(0, 0, 0, misc_ps)
                    if k == 14:
                        z_lo_part(0, 0, 1, u_ps)
                    if k == 17:
                        q_lo_part(0, 0, 0, misc_ps)

                def body(i, first, last):
                    for u in range(UN):
                        b = i * UN + u
                        old = not (first and u == 0)
                        new = not (last and u == UN - 1)
                        for t in range(QT):
                            if t == 5 and old:
                                finish(b - 1, 1 - u, 1)
                            row_max(b, t, u)
                            if t == 0 and not old:
                                close_ffn()
                                v.wait_ge(FF[0].res_done, NG)
                            if t < 2 and new:
                                stats(b + 1, t)
                            if t == 2 and old:
                                z_lo_part(b, u, 1, z_ps)
                                finish(b - 1, 1 - u, 0)
                            if t == 2 and new:
                                mean(b + 1)
                            if t == 3 and new:
                                norm_eps(A, b + 1, a_mv, QT, 0, a_mv[:, :, 1])
                            if t == (3 if old else 2):
                                q_lo_part(b, u, 1, q_ps)
                            if t == 3 and new:
                                normalise(b + 1, 1 - u, 0)
                            if t == 5 and new:
                                z_lo_part(b + 1, 1 - u, 0, misc_ps)
                                normalise(b + 1, 1 - u, 1)
                            if t == 7 and new:
                                q_lo_part(b + 1, 1 - u, 0, misc_ps)
                            if last:
                                start_ffn(u * QT + t)

                def run():
                    body(0, True, False)
                    with v.Fori(1, B // UN - 1) as i:
                        body(i, False, False)
                    body(B // UN - 1, False, True)
                    b, u = B - 1, (B - 1) % UN
                    start_ffn(16)
                    finish(b, u, 0)
                    for c in range(AHEAD):
                        lead_ffn(c)

                def end(k):
                    if k == 0:
                        finish(B - 1, (B - 1) % UN, 1)

                return begin, run, end

            opening0, _, _, run0, close0 = ffn(FF[0], 0)
            _, start1, lead1, run1, close1 = ffn(FF[1], 1)
            opening0()
            begin_attention, run_attention, end_attention = attention(close0, start1, lead1)
            run0(nothing, begin_attention)
            run_attention()
            run1(end_attention, nothing)
            close1()

        @block.tensor
        def _(pe):
            mm = nc.tensor.matmul

            def split3(out_, l_hi, l_lo, r_hi, r_lo, start=True, stop=True):
                mm(out_, l_hi, r_hi, start=start, stop=False)
                mm(out_, l_hi, r_lo, start=False, stop=False)
                return mm(out_, l_lo, r_hi, start=False, stop=stop)

            def weights_transpose(w):
                dst = wt_ps[w]
                if w == 0:
                    pe.wait_ge(w1_in, 32)
                if w == 2:
                    pe.wait_ge(w2_in, 32)
                if w < 2:
                    srcs = [w1_raw[:, 4 * w + c, :] for c in range(4)]
                elif w < 4:
                    srcs = [w2_raw[:, 4 * (w - 2) + c, :] for c in range(4)]
                else:
                    pe.wait_ge(small_in, 16 * 3)
                    srcs = [w1_raw[:, NC, :], w2_raw[:, NC, :], qk_raw[:, 0, :], qk_raw[:, 1, :]]
                for c, src in enumerate(srcs):
                    ins = nc.tensor.transpose(dst[:, c * P:(c + 1) * P], src, ident[:])
                ins.then_inc(wt_done, 1)

            def attention_matrix():
                mm(o_ps[1][:, 0:P], qkT[:, 0, :], qkT[:, 1, :], start=True, stop=True).then_inc(m_done, 1)

            def ffn(F, phase):
                def xn_transpose(g, dst):
                    pe.wait_ge(F.xn_done, g + 1)
                    pe.wait_ge(F.xn2_done, g + 1)
                    for t in range(TG):
                        ins = nc.tensor.transpose(dst[:, t * P:(t + 1) * P], xn[:, t, :], ident[:])
                    ins.then_inc(F.xnT_done, 1)

                def logits(g, u, dst):
                    pe.wait_ge(F.xf_done, g + 1)
                    wait(pe, F.sig_done, g)
                    for t in range(TG):
                        ins = mm(dst[:, t * E:(t + 1) * E], x_f[:, u, t * P:(t + 1) * P], wgT[:], start=True, stop=True)
                    ins.then_inc(F.lg_done, 1)

                def w_transpose(g, dst):
                    pe.wait_ge(F.scw_done, g + 1)
                    wait(pe, F.wT_done, g)
                    nc.tensor.transpose(dst[:, 0:P], scw[:].rearrange("p e t -> p (e t)"), ident[:]).then_inc(F.scwT_done, 1)

                def up(g, c, m, j, u):
                    if c == 0:
                        pe.wait_ge(F.xlo_done, g + 1)
                    wait(pe, F.s_done, m + 1 - HB)
                    split3(up_ps[j % HB], w1_hi[:, c, :], w1_lo[:, c, :], x_hi[:, u, :], x_lo[:, u, :]).then_inc(F.up_done, 1)

                def down(g, c, m, j, u):
                    if c == 0:
                        wait(pe, F.oT_copied, g - 1)
                    if c in WHOLE:
                        pe.wait_ge(F.sq_done, m + 1)
                        mm(o_ps[u], w2_f[:, WHOLE.index(c), :], g_f[:, j % RING, :], start=(c == 0),
                           stop=(c == NCH - 1)).then_inc(F.down_done, 1)
                        return
                    pe.wait_ge(F.glo_done, g * (NCH - len(WHOLE)) + sum(k not in WHOLE for k in range(c + 1)))
                    split3(o_ps[u], w2_hi[:, c, :], w2_lo[:, c, :], g_hi[:, j % RING, :], g_lo[:, j % RING, :],
                           start=(c == 0), stop=(c == NCH - 1)).then_inc(F.down_done, 1)

                def o_transpose(g, copied):
                    pe.wait_ge(F.oT_copied, g + 1)
                    pe.wait_ge(F.xf_done, copied)
                    wait(pe, F.res_done, g)
                    for t in range(TG):
                        ins = nc.tensor.transpose(tr_ps[:, t * P:(t + 1) * P], oT[:, t * P:(t + 1) * P], ident[:])
                    ins.then_inc(F.oTr_done, 1)

                def opening():
                    pe.wait_ge(const_done, 2)
                    pe.wait_ge(wg_in, 16)
                    nc.tensor.transpose(lg_ps[:, 0:E], wg_raw[:], ident[0:E, 0:E]).then_inc(wgT_done, 1)
                    xn_transpose(0, tr_ps)
                    pe.wait_ge(wgT_copied, 1)
                    logits(0, 0, lg_ps)
                    weights_transpose(0)
                    weights_transpose(1)
                    pe.wait_ge(F.xf_done, 1)
                    xn_transpose(1, tr_ps)
                    logits(1, 1, lg_ps)
                    weights_transpose(2)
                    weights_transpose(3)
                    w_transpose(0, wT_ps)
                    pe.wait_ge(F.xf_done, 2)
                    xn_transpose(2, tr_ps)
                    logits(2, 0, lg_ps)
                    weights_transpose(4)
                    pe.wait_ge(F.xf_done, 3)
                    xn_transpose(3, tr_ps)
                    pe.wait_ge(wt_hi, N_SETS)
                    pe.wait_ge(wt_lo, N_SETS)
                    attention_matrix()
                    for c in range(AHEAD - 1):
                        lead(c)
                    w_transpose(1, wT_ps)
                    pe.wait_ge(m_copied, 2)
                    lead(AHEAD - 1)

                def start(k):
                    for n in range(PREP):
                        if k == (2, 4, 10, 17)[n]:
                            pe.wait_ge(*((AT.pT_done, QT * (B - 2)), (F.sig_done, 1), (AT.pT_done, QT * (B - 1)), (AT.pT_done, QT * B))[n])
                            xn_transpose(n, tr_ps)
                        if n < 3 and k == (3, 5, 11)[n]:
                            logits(n, n % UN, tr_ps)
                    if k == 12:
                        pe.wait_ge(F.sig_done, 3)
                        w_transpose(0, tr_ps)
                    if k == 16:
                        w_transpose(1, wT_ps)

                def lead(c):
                    up(0, c, c, c, 0)

                def body(i, first, last, extra):
                    for u in range(UN):
                        g = i * UN + u
                        for c in range(NCH):
                            j = u * NCH + c
                            m = i * (UN * NCH) + j
                            if j + AHEAD < UN * NCH:
                                up(g + (c + AHEAD) // NCH, (c + AHEAD) % NCH, m + AHEAD, j + AHEAD, (j + AHEAD) // NCH)
                            elif not last:
                                up(g + 1, (c + AHEAD) % NCH, m + AHEAD, (j + AHEAD) % (UN * NCH), 0)
                            if c == 2 and not last:
                                logits(g + 3, 1 - u, lg_ps)
                            if c == 2 and not (first and u == 0):
                                o_transpose(g - 1, NG + 2 if last else g + PREP)
                            if c == 6 and not last:
                                w_transpose(g + 2, wT_ps)
                            if c == 7 and not last:
                                wait(pe, F.xf_done, g + PREP)
                                wait(pe, F.res_done, g)
                                xn_transpose(g + PREP, tr_ps)
                            down(g, c, m, j, u)
                            extra(j)

                def run(first_extra, last_extra):
                    if phase == 1:
                        pe.wait_ge(AT.pT_done, QT * B)
                    body(0, True, False, first_extra)
                    with pe.Fori(1, NG // UN - 1) as i:
                        body(i, False, False, nothing)
                    body(NG // UN - 1, False, True, last_extra)

                def close():
                    o_transpose(NG - 1, NG + 2)

                return opening, start, lead, run, close

            def attention(close_ffn, start_ffn, lead_ffn):
                A = AT
                N1 = FF[1]

                def z_transpose(b, u, half, dst):
                    pe.wait_ge(A.zn_done, 2 * b + half + 1)
                    for t in range(HQ):
                        ins = nc.tensor.transpose(dst[:, t * P:(t + 1) * P], zn[:, u, half * HQ + t, :], ident[:])
                    ins.then_inc(A.t_done, 1)

                def q_product(b, u, half, dst):
                    pe.wait_ge(A.zlo_done, 2 * b + half + 1)
                    cs = slice(half * 512, half * 512 + 512)
                    split3(dst, m_hi[:], m_lo[:], z_hi[:, u, cs], z_lo[:, u, cs]).then_inc(A.q_done, 1)

                def score(b, t, u):
                    if t % HQ == 0:
                        pe.wait_ge(A.qlo_done, 2 * b + t // HQ + 1)
                    wait(pe, A.exp_done, QT * b + t - 1)
                    dst = sc_ps[t % 2]
                    w = (t + 1) * P
                    qs = slice(t * P, (t + 1) * P)
                    for c0 in range(0, w, 512):
                        c1 = min(c0 + 512, w)
                        ins = split3(dst[:, c0:c1], q_hi[u][:, qs], q_lo[u][:, qs], z_hi[:, u, c0:c1], z_lo[:, u, c0:c1],
                                     stop=(c1 < w))
                    mm(dst[:, t * P:w], identb[:], maskb[:], start=False, stop=True).then_inc(A.sc_done, 1)

                def prob_transpose(b, t):
                    m = QT * b + t
                    pe.wait_ge(A.exp_done, m + 1)
                    wait(pe, A.pT_done, m)
                    if t == HQ and isinstance(b, int) and b >= B - 2:
                        pe.wait_ge(*((N1.sig_done, 2), (N1.wT_done, 1))[b - (B - 2)])
                    for k in range(t + 1):
                        ins = nc.tensor.transpose(tp_ps[:, k * P:(k + 1) * P], prob[:, t % PR, k * P:(k + 1) * P], ident[:])
                    ins.then_inc(A.tp_done, 1)

                def mix(b, u, half, k0, k1):
                    last = (half + 1) * HQ
                    if k0 == 0:
                        pe.wait_ge(A.pT_done, QT * b + last)
                        wait(pe, A.uT_done, 2 * b + half)
                    for k in range(k0, k1):
                        q0 = max(0, k - half * HQ) * P
                        ins = mm(u_ps[:, q0:], zn[:, u, k, :], pT[half][:, k, q0:], start=(k == 0), stop=(k == last - 1))
                    if k1 == last:
                        ins.then_inc(A.u_done, 1)

                def values(b, half):
                    pe.wait_ge(A.uT_done, 2 * b + half + 1)
                    if half == 0 and not (isinstance(b, int) and b == B - 1):
                        pe.wait_ge(A.qlo_done, 2 * b + 3)
                    else:
                        pe.wait_ge(A.fin_done, 2 * b + half)
                    for t in range(HQ):
                        ins = mm(misc_ps[:, t * P:(t + 1) * P], uT[:, half, t * P:(t + 1) * P], vw[:], start=True, stop=True)
                    ins.then_inc(A.out_done, 1)

                def begin(k):
                    if k == 10:
                        z_transpose(0, 0, 0, misc_ps)
                    if k == 12:
                        z_transpose(0, 0, 1, u_ps)
                    if k == 15:
                        q_product(0, 0, 0, misc_ps)

                def body(i, first, last):
                    for u in range(UN):
                        b = i * UN + u
                        old = not (first and u == 0)
                        new = not (last and u == UN - 1)
                        for t in range(QT):
                            if t == 0 and old:
                                prob_transpose(b - 1, QT - 2)
                            score(b, t, u)
                            if t == 7 and new:
                                q_product(b + 1, 1 - u, 0, misc_ps)
                            if t == 0 and not old:
                                close_ffn()
                            if t == 2 and not old:
                                pe.wait_ge(FF[0].res_done, NG)
                            if t >= 2:
                                prob_transpose(b, t - 2)
                            elif t == 1 and old:
                                prob_transpose(b - 1, QT - 1)
                            if t == 1 and old:
                                values(b - 1, 0)
                                pe.wait_ge(A.exp_done, QT * b)
                                z_transpose(b, u, 1, z_ps)
                            if t == (3 if old else 2):
                                pe.wait_ge(A.exp_done, QT * b + 1)
                                q_product(b, u, 1, q_ps)
                            if t == 2 and old:
                                mix(b - 1, 1 - u, 1, 0, HQ)
                            if t == 3 and old:
                                mix(b - 1, 1 - u, 1, HQ, QT)
                            if t == 4 and old:
                                values(b - 1, 1)
                            if t == 5 and new:
                                wait(pe, A.fin_done, 2 * b)
                                z_transpose(b + 1, 1 - u, 0, misc_ps)
                            if t == 7:
                                mix(b, u, 0, 0, HQ)
                            if last:
                                start_ffn(u * QT + t)

                def run():
                    pe.wait_ge(m_ready, 1)
                    body(0, True, False)
                    with pe.Fori(1, B // UN - 1) as i:
                        body(i, False, False)
                    body(B // UN - 1, False, True)
                    b, u = B - 1, (B - 1) % UN
                    prob_transpose(b, QT - 2)
                    values(b, 0)
                    pe.wait_ge(A.exp_done, QT * B)
                    lead_ffn(0)
                    prob_transpose(b, QT - 1)
                    start_ffn(16)
                    for c in range(1, AHEAD - 1):
                        lead_ffn(c)
                    pe.wait_ge(N1.wT_done, UN)
                    mix(b, u, 1, 0, QT)
                    start_ffn(17)
                    lead_ffn(AHEAD - 1)

                def end(k):
                    if k == 0:
                        values(B - 1, 1)
                    if k == 1:
                        pe.wait_ge(A.fin_done, 2 * B)

                return begin, run, end

            opening0, _, _, run0, close0 = ffn(FF[0], 0)
            _, start1, lead1, run1, close1 = ffn(FF[1], 1)
            opening0()
            begin_attention, run_attention, end_attention = attention(close0, start1, lead1)
            run0(nothing, begin_attention)
            run_attention()
            run1(end_attention, nothing)
            close1()


_INS = ["L0_attn_x", "L0_attn_Qw", "L0_attn_Kw", "L0_attn_Vw", "L0_ffn_Wg", "L0_ffn_bias_corr", "L0_ffn_W1", "L0_ffn_W2",
        "L0_ffn_Ws1", "L0_ffn_Ws2"]


def kernel(**inputs):
    import numpy as _np
    import concourse.bacc as _bacc
    from concourse import mybir as _mybir
    from concourse.bass_utils import run_bass_kernel_spmd as _run

    nc = _bacc.Bacc("TRN2", target_bir_lowering=False, num_devices=1)
    arrays, args = {}, []
    for name in _INS:
        a = _np.ascontiguousarray(inputs[name])
        arrays[f"in_{name}"] = a
        args.append(nc.dram_tensor(f"in_{name}", a.shape, _mybir.dt.from_np(a.dtype), kind="ExternalInput").ap())
    shape = inputs["L0_attn_x"].shape
    args.append(nc.dram_tensor("out", shape, _mybir.dt.float32, kind="ExternalOutput").ap())
    macaron_kernel(nc, *args)
    r = _run(nc, [arrays], core_ids=[0])
    return r.results[0]["out"]
```
